# Optimizing a Trainium2 kernel written in Bass

```python
import numpy as np
import jax
import jax.numpy as jnp

def _softmax(x, axis=-1):
    return jax.nn.softmax(x, axis=axis)

def _gelu(x):
    return jax.nn.gelu(x, approximate=True)

def _silu(x):
    return jax.nn.silu(x)

def _sigmoid(x):
    return jax.nn.sigmoid(x)

def _layernorm(x, axis=-1, eps=1e-05):
    m = jnp.mean(x, axis=axis, keepdims=True)
    v = jnp.var(x, axis=axis, keepdims=True)
    return (x - m) / jnp.sqrt(v + eps)

def _scatter_add(tgt, idx, src, axis=0):
    return tgt.at[idx].add(src)

def _segment_sum(src, seg, n):
    return jax.ops.segment_sum(src, seg, n)
kernel_name = 'mk_cond_resid_d2_seqx_r4_6290b4'

def setup_inputs(seed: int=0):
    np.random.seed(seed)
    _w = jnp.asarray

    def _rec_inputs():
        import jax
        import jax.numpy as jnp
        _rk = jax.random.key(seed)
        x = 7.22e-05 + 1 * jax.random.normal(jax.random.fold_in(_rk, 1), (8, 256, 1024), jnp.float32)
        _lenS = 256 - jax.random.randint(jax.random.fold_in(_rk, 7), (8,), 0, max(1, 256 // 4) + 1, jnp.int32)
        _lenS2 = 256 - jax.random.randint(jax.random.fold_in(_rk, 8), (8,), 0, max(1, 256 // 4) + 1, jnp.int32)
        itok_B_2_6 = jax.random.randint(jax.random.fold_in(_rk, 11), (8,), 2, 7, jnp.int32)
        itok_B_0_7 = jax.random.randint(jax.random.fold_in(_rk, 12), (8,), 0, 8, jnp.int32)
        return (x, itok_B_2_6, itok_B_0_7)
    x, itok_B_2_6, itok_B_0_7 = _rec_inputs()

    def _L0_cond_setup():
        import jax, jax.numpy as jnp
        import numpy as np
        B, N, H, F = (4, 128, 1024, 2752)
        L, R, RANK = (1, 16, 16)
        SCALE = 0.5
        key = jax.random.key(seed)
        ks = jax.random.split(key, 12)
        nrm = lambda k, shape, fan: jax.random.normal(k, shape, jnp.float32) * fan ** (-0.5)
        inp = {'x': jax.random.normal(ks[0], (B, N, H), jnp.float32), 'W_gate': nrm(ks[1], (F, H), H), 'W_up': nrm(ks[2], (F, H), H), 'W_down': nrm(ks[3], (H, F), F), 'A_gate': nrm(ks[4], (L, R, RANK, H), H), 'B_gate': nrm(ks[5], (L, R, F, RANK), RANK), 'A_up': nrm(ks[6], (L, R, RANK, H), H), 'B_up': nrm(ks[7], (L, R, F, RANK), RANK), 'A_down': nrm(ks[8], (L, R, RANK, F), F), 'B_down': nrm(ks[9], (L, R, H, RANK), RANK), 'lora_indices': jax.random.randint(ks[10], (B,), 0, R), 'layer_idx': 0}
        return inp
    _L0_cond_all = _L0_cond_setup()
    _L0_cond_in = {k: v for k, v in _L0_cond_all.items() if k in ('W_gate', 'W_up', 'W_down', 'A_gate', 'B_gate', 'A_up', 'B_up', 'A_down', 'B_down')}
    del _L0_cond_all

    def _L1_cond_setup():
        import jax, jax.numpy as jnp
        import numpy as np
        TOP_K = 2
        LANG_BIAS = 5.0
        SCALING = 32.0 / 16.0
        LANGUAGE_PAD_ID = -1
        key = jax.random.key(seed)
        ks = jax.random.split(key, 6)
        B, T, D, O, E, R = (4, 512, 1024, 1024, 8, 16)
        x = jax.random.normal(ks[0], (B, T, D), dtype=jnp.float32)
        language_ids = jax.random.randint(ks[1], (B,), 0, E).astype(jnp.int64)
        W = jax.random.normal(ks[2], (O, D), dtype=jnp.float32) * (1.0 / np.sqrt(D))
        Wr = jax.random.normal(ks[3], (E, D), dtype=jnp.float32) * (1.0 / np.sqrt(D))
        A = jax.random.normal(ks[4], (E, R, D), dtype=jnp.float32) * (1.0 / np.sqrt(D))
        Bm = jax.random.normal(ks[5], (O, R), dtype=jnp.float32) * 0.0
        Bm = jnp.broadcast_to(Bm, (E, O, R)) + jax.random.normal(ks[5], (E, O, R), dtype=jnp.float32) * 0.02
        return {'x': x, 'language_ids': language_ids, 'W': W, 'Wr': Wr, 'A': A, 'B': Bm}
    _L1_cond_all = _L1_cond_setup()
    _L1_cond_in = {k: v for k, v in _L1_cond_all.items() if k in ('W', 'Wr', 'A', 'B')}
    del _L1_cond_all
    return {'x': x, 'itok_B_2_6': itok_B_2_6, 'itok_B_0_7': itok_B_0_7, 'L0_cond_W_gate': _L0_cond_in['W_gate'], 'L0_cond_W_up': _L0_cond_in['W_up'], 'L0_cond_W_down': _L0_cond_in['W_down'], 'L0_cond_A_gate': _L0_cond_in['A_gate'], 'L0_cond_B_gate': _L0_cond_in['B_gate'], 'L0_cond_A_up': _L0_cond_in['A_up'], 'L0_cond_B_up': _L0_cond_in['B_up'], 'L0_cond_A_down': _L0_cond_in['A_down'], 'L0_cond_B_down': _L0_cond_in['B_down'], 'L1_cond_W': _L1_cond_in['W'], 'L1_cond_Wr': _L1_cond_in['Wr'], 'L1_cond_A': _L1_cond_in['A'], 'L1_cond_B': _L1_cond_in['B']}

def reference(x, itok_B_2_6, itok_B_0_7, L0_cond_W_gate, L0_cond_W_up, L0_cond_W_down, L0_cond_A_gate, L0_cond_B_gate, L0_cond_A_up, L0_cond_B_up, L0_cond_A_down, L0_cond_B_down, L1_cond_W, L1_cond_Wr, L1_cond_A, L1_cond_B):
    import jax
    import jax.numpy as jnp

    def _L0_cond_ref(x, W_gate, W_up, W_down, A_gate, B_gate, A_up, B_up, A_down, B_down, lora_indices, layer_idx):
        import jax, jax.numpy as jnp
        import numpy as np
        B, N, H, F = (4, 128, 1024, 2752)
        L, R, RANK = (1, 16, 16)
        SCALE = 0.5

        def lora_add(base, inp, A, B):
            Ab = A[layer_idx][lora_indices]
            Bb = B[layer_idx][lora_indices]
            t = jnp.einsum('bri,bni->bnr', Ab, inp)
            return base + jnp.einsum('bor,bnr->bno', Bb, t) * SCALE
        gate = lora_add(jnp.einsum('bnh,fh->bnf', x, W_gate), x, A_gate, B_gate)
        up = lora_add(jnp.einsum('bnh,fh->bnf', x, W_up), x, A_up, B_up)
        act = jax.nn.silu(gate) * up
        down = lora_add(jnp.einsum('bnf,hf->bnh', act, W_down), act, A_down, B_down)
        return down

    def _L1_cond_ref(x, language_ids, W, Wr, A, B):
        import jax, jax.numpy as jnp
        import numpy as np
        TOP_K = 2
        LANG_BIAS = 5.0
        SCALING = 32.0 / 16.0
        LANGUAGE_PAD_ID = -1
        base = jnp.einsum('btd,od->bto', x, W)
        E = Wr.shape[0]
        logits = jnp.einsum('btd,ed->bte', x.astype(jnp.float32), Wr.astype(jnp.float32))
        expert_targets = language_ids
        valid = expert_targets >= 0
        tgt = jnp.where(valid, expert_targets, 0)
        bias = jax.nn.one_hot(tgt, E, dtype=logits.dtype) * LANG_BIAS
        bias = jnp.where(valid[:, None], bias, 0.0)
        logits = logits + bias[:, None, :]
        topw, topi = jax.lax.top_k(logits, TOP_K)
        weights = jax.nn.softmax(topw, axis=-1)
        gates = jnp.sum(jax.nn.one_hot(topi, E, dtype=weights.dtype) * weights[..., None], axis=-2)
        gates = gates.astype(x.dtype)
        h = jnp.einsum('btd,erd->bter', x, A)
        lora_out = jnp.einsum('bter,bte,eor->bto', h, gates, B)
        return base + SCALING * lora_out
    x = x + _L0_cond_ref(x, L0_cond_W_gate, L0_cond_W_up, L0_cond_W_down, L0_cond_A_gate, L0_cond_B_gate, L0_cond_A_up, L0_cond_B_up, L0_cond_A_down, L0_cond_B_down, itok_B_2_6, 0)
    x = x + _L1_cond_ref(x, itok_B_0_7, L1_cond_W, L1_cond_Wr, L1_cond_A, L1_cond_B)
    return x

_drawn_inputs = setup_inputs


def setup_inputs(seed=0):
    import zlib

    import numpy as np

    out = dict(_drawn_inputs(seed))
    spreads = {}
    factors = {}
    for name, (base, spread) in spreads.items():
        noise = np.random.default_rng([zlib.crc32(name.encode()), seed]).standard_normal(out[name].shape)
        drawn = base * np.exp(spread * noise) if base else spread * noise
        out[name] = jnp.asarray(drawn.astype(out[name].dtype))
    for name, factor in factors.items():
        out[name] = (out[name] * factor).astype(out[name].dtype)
    return out
```

```python
from contextlib import ExitStack

import concourse.bass as bass
from concourse import mybir

P = 128
D = 1024
F = 2752
KT = D // P
FULL = F // P
TAIL = F - FULL * P
FT = FULL + 1
SEQ = 256
NSEQ = 8
HALVES = 2
SEQ_HALF = NSEQ // HALVES
CHUNKS = 2
CH = 2 * SEQ
NT = CHUNKS * CH
RANK = 16
ADAPTERS = 16
EXPERTS = 8
LANG_BIAS = 5.0
SCALING = 2.0
LORA_SCALE = 0.5
GU = 2 * FULL + 1
LB = GU + 1
BLOCKS = (FULL - 1) // 2

G_RANK, G_GATE0, G_BLOCK, PER_BLOCK = 0, 1, 2, 13
G_UP_A, G_GATE_B, G_UP_B, G_GATE_NEXT, G_LDOWN, G_DOWN = 0, 1, 2, 3, 4, 5
G_UP_LAST = G_BLOCK + PER_BLOCK * BLOCKS
G_TAIL = G_UP_LAST + 1
G_LDOWN_LAST = G_TAIL + 1
G_DOWN_LAST = G_LDOWN_LAST + 1
G_ROUTER = G_DOWN_LAST + KT
G_EXPERTS = G_ROUTER + 1
G_LOGITS_T = G_EXPERTS + 1
G_GATES_T = G_LOGITS_T + 1
G_OUT = G_GATES_T + 1
GROUPS = G_OUT + KT

S_RANK, S_GU0, S_BLOCK, STAGES_BLOCK = 0, 1, 4, 6
S_DOWN_LAST = S_BLOCK + STAGES_BLOCK * BLOCKS
S_DOWN_TAIL = S_DOWN_LAST + 1
S_BDOWN = S_DOWN_TAIL + 1
S_EXPERTS = S_BDOWN + 2
S_EXPERTS_B = S_EXPERTS + 1
S_OUT = S_EXPERTS_B + 1
STAGES = S_OUT + KT
RING = 3
LOADED = 96
assert STAGES % RING == 0 and LB % 2 == 0

USES = (2 * BLOCKS + 5, 2 * BLOCKS + 7, 5 * BLOCKS + 7, 4 * BLOCKS + 6)
RING3 = (2, 3, 1)
U_LDOWN_LAST = 5 * BLOCKS + 1
FIRST3 = {2: 5 * BLOCKS + 1, 3: 4 * BLOCKS, 1: 2 * BLOCKS + 1}
FIRST_OUT = {2: 5 * BLOCKS + 4, 3: 4 * BLOCKS + 3, 1: 2 * BLOCKS + 5}
U_EXPERTS = 2 * BLOCKS + 4
ROUTE_STEPS = 11

ALU = mybir.AluOpType
ACT = mybir.ActivationFunctionType
F32 = mybir.dt.float32
F32R = mybir.dt.float32r
I32 = mybir.dt.int32
U32 = mybir.dt.uint32

HI, LO = 0, 1
PASSES = ((HI, HI), (HI, LO), (LO, HI))
RANK_PASSES = (HI, LO)


def cond_resid_kernel(nc, x_t, w_gu, w_down, a_gu, b_gu, a_down, b_down, w_out, a_exp, b_exp, w_route,
                      adapter_of, language_of, identity, seq_scale, expert_no, out):
    with ExitStack() as ctx:
        def sb(name, shape, dt=F32):
            return ctx.enter_context(nc.sbuf_tensor(name, shape, dt))

        def sem(name):
            return ctx.enter_context(nc.semaphore(name))

        lb_dram = nc.dram_tensor("lb_dram", (HALVES, LB, 2 * RANK, CHUNKS, P), F32).ap()

        xs = [sb("x_hi", [P, KT, NT], F32R), sb("x_lo", [P, KT, NT], F32R)]
        resid = sb("resid", [P, KT, NT])
        act = sb("act", [P, 2, 2, NT], F32R)
        wd = sb("wd", [P, 2, 2, D], F32R)
        ad = sb("ad", [P, 2, P], F32R)
        wt = sb("wt", [P, 2, 2, KT, P], F32R)
        stage = sb("stage", [P, RING, D])
        lb_raw = sb("lb_raw", [3 * 2 * RANK, 2, CHUNKS, P])
        lbw = sb("lbw", [3 * 2 * RANK, 2, CHUNKS, P], F32R)
        ranks = sb("ranks", [3 * 2 * RANK, CHUNKS, 2, CH], F32R)
        ldown = sb("ldown", [P, CH])
        ad_raw = sb("ad_raw", [P, SEQ_HALF, FT, RANK])
        tmp_s = sb("tmp_s", [P, CHUNKS, CH])
        tmp_p = sb("tmp_p", [P, CHUNKS, CH])
        route_raw = sb("route_raw", [P, KT, EXPERTS])
        route_w = sb("route_w", [P, KT, 2, EXPERTS], F32R)
        ident = sb("ident", [P, P])
        scale_of = sb("scale_of", [P, 2])
        expert = sb("expert", [P, EXPERTS])
        adapters = sb("adapters", [1, NSEQ], I32)
        lang_i = sb("lang_i", [P, NSEQ], I32)
        lang = sb("lang", [P, NSEQ])
        lang_bias = sb("lang_bias", [P, NSEQ, EXPERTS])
        TT = NT // P
        logits2 = sb("logits2", [P, TT, 2, EXPERTS])
        logits = sb("logits", [P, TT, EXPERTS])
        best = sb("best", [P, TT, 8])
        best_at = sb("best_at", [P, TT, 8], U32)
        best_no = sb("best_no", [P, TT, 2])
        highest = sb("highest", [P, TT])
        odds = sb("odds", [P, 2, TT])
        weight = sb("weight", [P, 4, TT])
        picked = sb("picked", [P, 2, TT, EXPERTS])

        pair = [ctx.enter_context(nc.psum_tensor(f"pair{i}", [P, CHUNKS, CH], F32)) for i in range(4)]

        const_in = sem("const_in")
        lb_gathered = sem("lb_gathered")
        stage_in = [sem(f"stage_in{i}") for i in range(RING)]
        lb_in = [sem(f"lb_in{i}") for i in range(2)]
        ad_in = sem("ad_in")
        x_in = [sem(f"x_in{k}") for k in range(KT)]
        out_stored = [sem(f"out_stored{k}") for k in range(KT)]
        rounded = sem("rounded")
        split = sem("split")
        lb_rounded = sem("lb_rounded")
        lb_split = sem("lb_split")
        x_rounded = sem("x_rounded")
        x_split = sem("x_split")
        groups_done = sem("groups_done")
        pair_free = [sem(f"pair_free{i}") for i in range(4)]
        act_rounded = sem("act_rounded")
        act_split = sem("act_split")
        tail_product = sem("tail_product")
        ldown_cleared = sem("ldown_cleared")
        lora_lo = sem("lora_lo")
        lora_sum = sem("lora_sum")
        lora_rounded = sem("lora_rounded")
        lora_split = sem("lora_split")
        route_rounded = sem("route_rounded")
        route_ready = sem("route_ready")
        lang_ready = sem("lang_ready")
        bias_ready = sem("bias_ready")
        route_step = sem("route_step")
        exp_ready = sem("exp_ready")
        hg_rounded = sem("hg_rounded")
        hg_split = sem("hg_split")

        def done(half, group, chunk=1):
            return 2 * GROUPS * half + (2 * GROUPS + 2 * group + chunk + 1)

        def done_last_half(half, group):
            return 2 * GROUPS * half + (2 * group + 2)

        def freed(p, half, use, chunk=1):
            return 2 * USES[p] * half + 2 * use + (chunk + 3)

        def free_for(p, half, use, chunk=1):
            return 2 * USES[p] * half + 2 * use + (chunk + 1)

        block = ctx.enter_context(nc.Block())

        @block.gpsimd
        def _(pool):
            pool.dma_start(adapters[:, :], adapter_of).then_inc(const_in, 16)
            pool.dma_start(lang_i[:, :], language_of.to_broadcast([P, NSEQ])).then_inc(const_in, 16)
            pool.dma_start(ident[:, :], identity).then_inc(const_in, 16)
            pool.dma_start(scale_of[:, :], seq_scale).then_inc(const_in, 16)
            pool.dma_start(expert[:, :], expert_no).then_inc(const_in, 16)
            pool.dma_start(route_raw[:, :, :], w_route).then_inc(const_in, 16)

            def load_x(half):
                for k in range(KT):
                    if half:
                        pool.wait_ge(out_stored[k], 16 * half)
                    pool.dma_start(resid[:, k, :], x_t[half, k]).then_inc(x_in[k], 16)

            def gather_lb(half):
                for s in range(SEQ_HALF):
                    chunk, b = divmod(s, 2)
                    n = half * SEQ_HALF + s
                    a = pool.value_load(adapters[0:1, n:n + 1], min_val=0, max_val=ADAPTERS - 1)
                    src = b_gu[bass.ds(a, 1)].rearrange("o r t f -> (o r) t f")
                    dst = lb_dram[half, :, b * RANK:(b + 1) * RANK, chunk, :].rearrange("t r f -> r t f")
                    pool.dma_start(dst, src).then_inc(lb_gathered, 16)
                pool.wait_ge(lb_gathered, 16 * SEQ_HALF * (half + 1))

            def store_out(half):
                for o in range(KT):
                    p = RING3[o % 3]
                    pool.wait_ge(pair_free[p], freed(p, half, FIRST_OUT[p] + o // 3))
                    pool.dma_start(out[half, o], resid[:, o, :]).then_inc(out_stored[o], 16)

            load_x(0)
            pool.wait_ge(const_in, 16 * 6)
            pool.wait_ge(x_in[KT - 4], 16)
            gather_lb(0)
            gather_lb(1)
            store_out(0)
            load_x(1)
            store_out(1)
            for k in range(KT):
                pool.wait_ge(out_stored[k], 16 * HALVES)

        @block.sync
        def _(sp):
            sp.wait_ge(const_in, 16 * 6)
            with sp.Fori(0, HALVES) as half:
                stage0 = STAGES * half

                def slot_free(n):
                    sp.wait_ge(split, n + 1)

                def adapter(s):
                    return sp.value_load(adapters[0:1, bass.ds(SEQ_HALF * half + s, 1)],
                                         min_val=0, max_val=ADAPTERS - 1)

                def load(k, base, src):
                    slot_free(base + k)
                    sp.dma_start(stage[:, k % RING, :], src).then_inc(stage_in[k % RING], LOADED)

                def load_lb(e):
                    sp.wait_ge(lb_split, LB * half + e + 1)
                    return e

                def lb_dmas(slot, e):
                    for part in range(3):
                        rows = slice(part * 2 * RANK, (part + 1) * 2 * RANK)
                        sp.dma_start(lb_raw[rows, slot, :, :],
                                     lb_dram[bass.ds(half, 1), bass.ds(e, 1)].rearrange("a b r c f -> (a b r) c f")
                                     ).then_inc(lb_in[slot], 16)

                def one(t, n):
                    return t[bass.ds(n, 1)].rearrange("o p n -> (o p) n")

                of = [adapter(s) for s in range(SEQ_HALF)]
                slot_free(stage0)
                for s in range(SEQ_HALF):
                    sp.dma_start(stage[:, 0, s * 256:(s + 1) * 256], one(a_gu, of[s])
                                 ).then_inc(stage_in[0], 32 if s % 2 else 16)
                load(S_GU0, stage0, w_gu[0])
                for s in range(SEQ_HALF):
                    sp.dma_start(ad_raw[:, s, :, :].rearrange("p t r -> p (t r)"), one(a_down, of[s])
                                 ).then_inc(ad_in, 16)
                load(S_GU0 + 1, stage0, w_gu[1])
                sp.wait_ge(lb_gathered, 16 * SEQ_HALF * half + 16 * SEQ_HALF)
                for e in range(3):
                    load_lb(e)
                    lb_dmas(e % 2, e)
                    if e == 0:
                        load(S_GU0 + 2, stage0, w_gu[2])

                with sp.Fori(0, BLOCKS) as blk:
                    base = stage0 + STAGES_BLOCK * blk
                    tile = 4 * blk
                    load(S_BLOCK + 0, base, one(w_down, 2 * blk))
                    load(S_BLOCK + 1, base, one(w_gu, tile + 3))
                    load_lb(tile + 3)
                    lb_dmas(1, tile + 3)
                    load(S_BLOCK + 2, base, one(w_gu, tile + 4))
                    load_lb(tile + 4)
                    lb_dmas(0, tile + 4)
                    load(S_BLOCK + 3, base, one(w_down, 2 * blk + 1))
                    load(S_BLOCK + 4, base, one(w_gu, tile + 5))
                    load_lb(tile + 5)
                    lb_dmas(1, tile + 5)
                    load(S_BLOCK + 5, base, one(w_gu, tile + 6))
                    load_lb(tile + 6)
                    lb_dmas(0, tile + 6)

                load(S_DOWN_LAST, stage0, w_down[FULL - 1])
                load_lb(LB - 1)
                lb_dmas(1, LB - 1)
                load(S_DOWN_TAIL, stage0, w_down[FULL])
                for chunk in range(CHUNKS):
                    n = S_BDOWN + chunk
                    slot_free(stage0 + n)
                    for b in range(2):
                        for part in range(3):
                            row = part * 2 * RANK + b * RANK
                            sp.dma_start(stage[row:row + RANK, n % RING, :], one(b_down, of[2 * chunk + b])
                                         ).then_inc(stage_in[n % RING], 16)
                load(S_EXPERTS, stage0, a_exp)
                load(S_EXPERTS_B, stage0, b_exp)
                for o in range(KT):
                    load(S_OUT + o, stage0, w_out[o])

        @block.tensor
        def _(pe):
            pe.sem_inc(groups_done, 2 * GROUPS)
            with pe.Fori(0, HALVES) as half:

                def stages_ready(n):
                    pe.wait_ge(split, STAGES * half + n + (RING + 1))

                def bank_free(p, use, chunk):
                    pe.wait_ge(pair_free[p], free_for(p, half, use, chunk))

                def columns(chunk):
                    return slice(chunk * CH, (chunk + 1) * CH)

                def width_product(p, use, slot, stop, also_wait=None):
                    for chunk in range(CHUNKS):
                        bank_free(p, use, chunk)
                    for k in range(KT):
                        if also_wait and k == KT // 2:
                            also_wait()
                        for w, a in PASSES:
                            for chunk in range(CHUNKS):
                                last = stop and k == KT - 1 and w == LO
                                mm = nc.tensor.matmul(pair[p][:, chunk, :], wt[:, slot, w, k, :],
                                                      xs[a][:, k, columns(chunk)],
                                                      start=(k == 0 and w == HI and a == HI), stop=last)
                                if last:
                                    mm.then_inc(groups_done, 1)

                def lora_tile(p, e, slot, side, last=True):
                    pe.wait_ge(lb_split, LB * half + e + 3)
                    for chunk in range(CHUNKS):
                        mm = nc.tensor.matmul(pair[p][:, chunk, :], lbw[:, slot, chunk, :],
                                              ranks[:, chunk, side, :], start=False, stop=last)
                        if last:
                            mm.then_inc(groups_done, 1)

                def gate_or_up(p, use, n, e, side):
                    stages_ready(n)
                    width_product(p, use, 1 - side, stop=False)
                    lora_tile(p, e, side, side)

                def down_product(p, h, first, tail, stop):
                    for t in range(2):
                        if not (t and tail):
                            parts = [(wd[:, t, w, h * P:(h + 1) * P], act[:, t, a]) for w, a in PASSES]
                        else:
                            parts = [(wd[:, t, HI, h * P:(h + 1) * P], act[:, t, HI]),
                                     (wd[0:TAIL, t, LO, h * P:(h + 1) * P], act[0:TAIL, t, HI])]
                        for i, (weights, values) in enumerate(parts):
                            for chunk in range(CHUNKS):
                                last = stop and t == 1 and i == len(parts) - 1
                                mm = nc.tensor.matmul(pair[p][:, chunk, :], weights, values[:, columns(chunk)],
                                                      start=(first and t == 0 and i == 0), stop=last)
                                if last:
                                    mm.then_inc(groups_done, 1)

                def lora_down(p, tail):
                    for t in range(2):
                        for a in RANK_PASSES[:1 if t and tail else 2]:
                            for chunk in range(CHUNKS):
                                last = t == 1 and (tail or a == LO)
                                mm = nc.tensor.matmul(pair[p][:, chunk, :], ad[:, t, :], act[:, t, a, columns(chunk)],
                                                      start=(t == 0 and a == HI), stop=last)
                                if last:
                                    mm.then_inc(groups_done, 1)

                stages_ready(S_RANK)
                for chunk in range(CHUNKS):
                    bank_free(2, 0, chunk)
                rank_w = wt[:, 0, :, :, :].rearrange("p c k m -> p (c k) m")
                for k in range(KT):
                    pe.wait_ge(x_split, 2 * KT * half + k + 1)
                    for a in RANK_PASSES:
                        for chunk in range(CHUNKS):
                            mm = nc.tensor.matmul(pair[2][:, chunk, :], rank_w[:, chunk * KT + k, :],
                                                  xs[a][:, k, columns(chunk)],
                                                  start=(k == 0 and a == HI), stop=(k == KT - 1 and a == LO))
                            if k == KT - 1 and a == LO:
                                mm.then_inc(groups_done, 1)
                stages_ready(S_GU0)
                width_product(0, 0, 1, stop=False)
                pe.wait_ge(lora_split, 4 * half + 2)
                lora_tile(0, 0, 0, 0)

                with pe.Fori(0, BLOCKS) as blk:
                    st = STAGES_BLOCK * blk
                    gate_or_up(1, 2 * blk, S_GU0 + 1 + st, 4 * blk + 1, 1)
                    gate_or_up(0, 2 * blk + 1, S_GU0 + 2 + st, 4 * blk + 2, 0)
                    gate_or_up(1, 2 * blk + 1, S_BLOCK + 1 + st, 4 * blk + 3, 1)
                    gate_or_up(0, 2 * blk + 2, S_BLOCK + 2 + st, 4 * blk + 4, 0)
                    stages_ready(S_BLOCK + 3 + st)
                    pe.wait_ge(act_split, 4 * (BLOCKS + 1) * half + 4 * blk + 4)
                    for g in range(1 + KT):
                        p, use = (2, 5 * blk + 1 + g // 2) if g % 2 == 0 else (3, 4 * blk + g // 2)
                        for chunk in range(CHUNKS):
                            bank_free(p, use, chunk)
                        if g == 0:
                            lora_down(p, tail=False)
                        else:
                            down_product(p, g - 1, first=True, tail=False, stop=True)

                gate_or_up(1, 2 * BLOCKS, S_DOWN_LAST - 2, LB - 3, 1)
                stages_ready(S_DOWN_LAST - 1)
                width_product(0, 2 * BLOCKS + 1, 1, stop=False)
                lora_tile(0, LB - 2, 0, 0, last=False)
                lora_tile(0, LB - 1, 1, 1)
                stages_ready(S_DOWN_TAIL)
                pe.wait_ge(act_split, 4 * (BLOCKS + 1) * half + 4 * (BLOCKS + 1))
                for chunk in range(CHUNKS):
                    bank_free(2, U_LDOWN_LAST, chunk)
                lora_down(2, tail=True)
                b_down_w = wt[0:3 * 2 * RANK, 0, :, :, :].rearrange("p c k m -> p c (k m)")

                def last_down(h):
                    if h == 0:
                        stages_ready(S_BDOWN + 1)
                        pe.wait_ge(lora_split, 4 * half + 4)
                    for chunk in range(CHUNKS):
                        nc.tensor.matmul(pair[RING3[(h + 1) % 3]][:, chunk, :],
                                         b_down_w[:, chunk, h * P:(h + 1) * P], ranks[:, chunk, 0, :],
                                         start=False, stop=True).then_inc(groups_done, 1)

                for h in range(KT):
                    p = RING3[(h + 1) % 3]
                    for chunk in range(CHUNKS):
                        bank_free(p, FIRST3[p] + (h + 1) // 3, chunk)
                    down_product(p, h, first=True, tail=True, stop=False)
                    if h:
                        last_down(h - 1)
                last_down(KT - 1)

                pe.wait_ge(route_ready, 1)
                for chunk in range(CHUNKS):
                    bank_free(0, 2 * BLOCKS + 2, chunk)
                for k in range(KT):
                    pe.wait_ge(x_split, 2 * KT * half + KT + k + 1)
                    for a in RANK_PASSES:
                        for chunk in range(CHUNKS):
                            last = k == KT - 1 and a == LO
                            mm = nc.tensor.matmul(pair[0][0:2 * EXPERTS, chunk, :],
                                                  route_w[:, k, :, :].rearrange("p a e -> p (a e)"),
                                                  xs[a][:, k, columns(chunk)],
                                                  start=(k == 0 and a == HI), stop=last)
                            if last:
                                mm.then_inc(groups_done, 1)
                stages_ready(S_EXPERTS)
                width_product(1, U_EXPERTS, 1, stop=True, also_wait=lambda: bank_free(0, 2 * BLOCKS + 3, 1))
                per_chunk = TT // CHUNKS
                for chunk in range(CHUNKS):
                    for t in range(per_chunk):
                        mm = nc.tensor.transpose(pair[0][:, chunk, t * 2 * EXPERTS:(t + 1) * 2 * EXPERTS],
                                                 tmp_s[0:2 * EXPERTS, chunk, t * P:(t + 1) * P],
                                                 ident[0:2 * EXPERTS, 0:2 * EXPERTS])
                    mm.then_inc(groups_done, 1)

                def out_main(o):
                    p = RING3[o % 3]
                    stages_ready(S_OUT + o)
                    width_product(p, FIRST_OUT[p] + o // 3, o % 2, stop=False)

                def out_lora(o):
                    p = RING3[o % 3]
                    if o == 0:
                        pe.wait_ge(hg_split, 2 * half + 2)
                    for w, a in PASSES:
                        for chunk in range(CHUNKS):
                            mm = nc.tensor.matmul(pair[p][:, chunk, :], wd[:, 0, w, o * P:(o + 1) * P],
                                                  act[:, 0, a, columns(chunk)], start=False, stop=(w == LO))
                            if w == LO:
                                mm.then_inc(groups_done, 1)

                out_main(0)
                pe.wait_ge(route_step, ROUTE_STEPS * half + ROUTE_STEPS)
                for chunk in range(CHUNKS):
                    bank_free(0, 2 * BLOCKS + 4, chunk)
                for chunk in range(CHUNKS):
                    for t in range(per_chunk):
                        mm = nc.tensor.transpose(pair[0][:, chunk, t * P:(t + 1) * P],
                                                 tmp_p[:, chunk, t * P:(t + 1) * P], ident[:, :])
                    mm.then_inc(groups_done, 1)
                for o in range(1, KT):
                    out_main(o)
                    out_lora(o - 1)
                out_lora(KT - 1)

        @block.scalar
        def _(sc):
            def copy(dst, src, **kw):
                return nc.scalar.activation(dst, src, ACT.Copy, **kw)

            sc.sem_inc(pair_free[0], 2)
            sc.wait_ge(const_in, 16 * 6)
            copy(route_w[:, :, HI, :], route_raw[:, :, :]).then_inc(route_rounded, 1)
            with sc.Fori(0, HALVES) as half:
                stage0 = STAGES * half

                def arrived(k, base):
                    h, blk = base
                    sc.wait_ge(stage_in[k % RING],
                               LOADED * (STAGES // RING) * h + LOADED * (STAGES_BLOCK // RING) * blk
                               + LOADED * (k // RING + 1))

                def round_wt(k, blk, slot, free_at):
                    sc.wait_ge(groups_done, free_at)
                    arrived(k, (half, blk))
                    copy(wt[:, slot, HI, :, :].rearrange("p k m -> p (k m)"), stage[:, k % RING, :]
                         ).then_inc(rounded, 1)

                def round_lb(slot, e, in_count):
                    sc.wait_ge(lb_in[slot], in_count)
                    copy(lbw[:, slot, :, :], lb_raw[:, slot, :, :]).then_inc(lb_rounded, 1)

                def lb_count(e_half, blk=0):
                    return 48 * (LB // 2) * half + 48 * 2 * blk + 48 * (e_half // 2 + 1)

                def round_wd(k, blk, t, free_at, tile):
                    sc.wait_ge(groups_done, free_at)
                    arrived(k, (half, blk))
                    copy(wd[:, t, HI, :], stage[:, k % RING, :])
                    sc.wait_ge(ad_in, 64 * half + 64)
                    copy(ad[:, t, :].rearrange("p (c a b r) -> p c a b r", c=CHUNKS, a=2, b=2)[:, :, HI, :, :],
                         ad_raw[:, :, bass.ds(tile, 1), :].rearrange("p (c b) o r -> p c b (o r)", c=CHUNKS)
                         ).then_inc(rounded, 1)

                def silu(group, use, s_free):
                    for chunk in range(CHUNKS):
                        sc.wait_ge(groups_done, done(half, group, chunk))
                        sc.wait_ge(pair_free[1], free_for(1, half, s_free, chunk))
                        nc.scalar.activation(tmp_s[:, chunk, :], pair[0][:, chunk, :], ACT.Silu
                                             ).then_inc(pair_free[0], 1)

                def round_act(t, up_use):
                    for chunk in range(CHUNKS):
                        sc.wait_ge(pair_free[1], freed(1, half, up_use, chunk))
                        copy(act[:, t, HI, chunk * CH:(chunk + 1) * CH], tmp_p[:, chunk, :]
                             ).then_inc(act_rounded, 1)

                sc.wait_ge(groups_done, done_last_half(half, G_GATES_T + KT - 2))
                arrived(S_RANK, (half, 0))
                rank_w = wt[:, 0, :, :, :].rearrange("p c k (a g b r) -> p c k a g b r", a=2, g=2, b=2)
                raw = stage[:, 0, :].rearrange("p (c b k g r) -> p c b k g r", c=CHUNKS, b=2, k=KT, g=2)
                for chunk in range(CHUNKS):
                    for b in range(2):
                        last = copy(rank_w[:, chunk, :, HI, :, b, :], raw[:, chunk, b, :, :, :])
                last.then_inc(rounded, 1)
                sc.wait_ge(groups_done, done_last_half(half, G_GATES_T + KT - 1))
                for k in range(KT):
                    sc.wait_ge(x_in[k], 16 * half + 16)
                    copy(xs[HI][:, k, :], resid[:, k, :]).then_inc(x_rounded, 1)
                round_wt(S_GU0, 0, 1, done_last_half(half, G_GATES_T + KT - 1))
                for chunk in range(CHUNKS):
                    sc.wait_ge(groups_done, done(half, G_RANK, chunk))
                    for b in range(2):
                        cols = slice(b * SEQ, (b + 1) * SEQ)
                        last = copy(tmp_s[0:64, chunk, cols], pair[2][64:128, chunk, cols],
                                    scale=scale_of[64:128, b:b + 1])
                    last.then_inc(lora_lo, 1)
                for chunk in range(CHUNKS):
                    sc.wait_ge(pair_free[2], freed(2, half, 0, chunk))
                    copy(ranks[0:32, chunk, 0, :], tmp_p[0:32, chunk, :])
                    copy(ranks[64:96, chunk, 0, :], tmp_p[0:32, chunk, :])
                    copy(ranks[32:64, chunk, 1, :], tmp_p[32:64, chunk, :])
                    copy(ranks[64:96, chunk, 1, :], tmp_p[32:64, chunk, :]).then_inc(lora_rounded, 1)
                round_wt(S_GU0 + 1, 0, 0, done(half, G_RANK))
                round_lb(0, 0, lb_count(0))
                round_lb(1, 1, lb_count(1))
                silu(G_GATE0, 0, 0)
                round_wt(S_GU0 + 2, 0, 1, done(half, G_GATE0))
                round_lb(0, 2, lb_count(2))

                with sc.Fori(0, BLOCKS) as blk:
                    g = PER_BLOCK * blk + G_BLOCK
                    round_wd(S_BLOCK, blk, 0, done(half, g - 1), 2 * blk)
                    round_act(0, 2 * blk)
                    round_wt(S_BLOCK + 1, blk, 0, done(half, g + G_UP_A))
                    round_lb(1, 3, lb_count(3, blk))
                    silu(g + G_GATE_B, 2 * blk + 1, 2 * blk + 1)
                    round_wt(S_BLOCK + 2, blk, 1, done(half, g + G_GATE_B))
                    round_lb(0, 4, lb_count(4, blk))
                    round_wd(S_BLOCK + 3, blk, 1, done(half, g - 1), 2 * blk + 1)
                    round_act(1, 2 * blk + 1)
                    round_wt(S_BLOCK + 4, blk, 0, done(half, g + G_UP_B))
                    round_lb(1, 5, lb_count(5, blk))
                    silu(g + G_GATE_NEXT, 2 * blk + 2, 2 * blk + 2)
                    round_wt(S_BLOCK + 5, blk, 1, done(half, g + G_GATE_NEXT))
                    round_lb(0, 6, lb_count(6, blk))

                round_wd(S_DOWN_LAST, 0, 0, done(half, G_UP_LAST - 1), FULL - 1)
                round_act(0, 2 * BLOCKS)
                sc.wait_ge(groups_done, done(half, G_UP_LAST))
                round_lb(1, LB - 1, lb_count(LB - 1))
                round_wd(S_DOWN_TAIL, 0, 1, done(half, G_UP_LAST - 1), FULL)
                b_down_w = wt[0:3 * 2 * RANK, 0, :, :, :].rearrange("p c k m -> p c (k m)")
                for chunk in range(CHUNKS):
                    arrived(S_BDOWN + chunk, (half, 0))
                    copy(b_down_w[:, chunk, :], stage[0:3 * 2 * RANK, (S_BDOWN + chunk) % RING, :]
                         ).then_inc(rounded, 1)
                for chunk in range(CHUNKS):
                    sc.wait_ge(groups_done, done(half, G_TAIL, chunk))
                    sc.wait_ge(act_split, 4 * (BLOCKS + 1) * half + 4 * BLOCKS + chunk + 1)
                    nc.scalar.activation(tmp_s[0:TAIL, chunk, :], pair[0][0:TAIL, chunk, :], ACT.Silu)
                    copy(tmp_p[0:TAIL, chunk, :], pair[0][TAIL:2 * TAIL, chunk, :]).then_inc(pair_free[0], 1)
                for chunk in range(CHUNKS):
                    sc.wait_ge(tail_product, 2 * half + chunk + 1)
                    copy(act[0:TAIL, 1, HI, chunk * CH:(chunk + 1) * CH], tmp_p[0:TAIL, chunk, :]
                         ).then_inc(act_rounded, 1)
                round_wt(S_EXPERTS, 0, 1, done(half, G_TAIL))
                for chunk in range(CHUNKS):
                    rows, low = slice(64 * chunk, 64 * chunk + 32), slice(64 * chunk + 32, 64 * chunk + 64)
                    sc.wait_ge(pair_free[2], freed(2, half, U_LDOWN_LAST, chunk))
                    for b in range(2):
                        cols = slice(b * SEQ, (b + 1) * SEQ)
                        last = copy(tmp_s[rows, chunk, cols], ldown[low, cols], scale=scale_of[low, b:b + 1])
                    last.then_inc(lora_lo, 1)
                for chunk in range(CHUNKS):
                    rows = slice(64 * chunk, 64 * chunk + 32)
                    sc.wait_ge(lora_sum, 2 * half + chunk + 1)
                    copy(ranks[0:32, chunk, 0, :], tmp_p[rows, chunk, :])
                    copy(ranks[64:96, chunk, 0, :], tmp_p[rows, chunk, :]).then_inc(lora_rounded, 1)
                for k in range(KT):
                    p = RING3[(k + 1) % 3]
                    sc.wait_ge(pair_free[p], freed(p, half, FIRST3[p] + (k + 1) // 3))
                    copy(xs[HI][:, k, :], resid[:, k, :]).then_inc(x_rounded, 1)
                sc.wait_ge(groups_done, done(half, G_DOWN_LAST + KT - 1))
                arrived(S_EXPERTS_B, (half, 0))
                copy(wd[:, 0, HI, :], stage[:, S_EXPERTS_B % RING, :]).then_inc(rounded, 1)
                round_wt(S_OUT, 0, 0, done(half, G_DOWN_LAST + KT - 1))
                for chunk in range(CHUNKS):
                    sc.wait_ge(groups_done, done(half, G_ROUTER, chunk))
                    copy(tmp_s[0:2 * EXPERTS, chunk, :], pair[0][0:2 * EXPERTS, chunk, :]).then_inc(pair_free[0], 1)
                round_wt(S_OUT + 1, 0, 1, done(half, G_EXPERTS))
                per_chunk = TT // CHUNKS
                for chunk in range(CHUNKS):
                    sc.wait_ge(groups_done, done(half, G_LOGITS_T, chunk))
                    copy(logits2[:, chunk * per_chunk:(chunk + 1) * per_chunk, :, :].rearrange("p t a e -> p (t a e)"),
                         pair[0][:, chunk, 0:per_chunk * 2 * EXPERTS]).then_inc(pair_free[0], 1)
                sc.wait_ge(route_step, ROUTE_STEPS * half + 4)
                nc.scalar.activation(odds[:, 1, :], odds[:, 0, :], ACT.Exp).then_inc(exp_ready, 1)
                for chunk in range(CHUNKS):
                    sc.wait_ge(groups_done, done(half, G_GATES_T, chunk))
                    copy(tmp_s[:, chunk, :], pair[0][:, chunk, :]).then_inc(pair_free[0], 1)
                round_wt(S_OUT + 2, 0, 0, done(half, G_GATES_T))
                for chunk in range(CHUNKS):
                    sc.wait_ge(pair_free[1], freed(1, half, U_EXPERTS, chunk))
                    copy(act[:, 0, HI, chunk * CH:(chunk + 1) * CH], tmp_p[:, chunk, :]).then_inc(hg_rounded, 1)
                for o in range(3, KT):
                    round_wt(S_OUT + o, 0, o % 2, done(half, G_GATES_T + o - 2))

        @block.vector
        def _(dve):
            def rest(dst, whole, high):
                return nc.vector.tensor_tensor(dst, whole, high.bitcast(F32), ALU.subtract)

            dve.sem_inc(split, RING)
            dve.sem_inc(lb_split, 2)
            for p in range(1, 4):
                dve.sem_inc(pair_free[p], 2)
            dve.wait_ge(const_in, 16 * 6)
            nc.vector.tensor_copy(lang[:, :], lang_i[:, :]).then_inc(lang_ready, 1)
            dve.wait_ge(lang_ready, 1)
            for n in range(NSEQ):
                last = nc.vector.tensor_scalar(lang_bias[:, n, :], expert[:, :], lang[:, n:n + 1], LANG_BIAS,
                                               ALU.is_equal, ALU.mult)
            last.then_inc(bias_ready, 1)
            dve.wait_ge(route_rounded, 1)
            rest(route_w[:, :, LO, :], route_raw[:, :, :], route_w[:, :, HI, :]).then_inc(route_ready, 1)

            with dve.Fori(0, HALVES) as half:
                stage0 = STAGES * half

                def rest_wt(k, n, slot):
                    dve.wait_ge(rounded, stage0 + n + 1)
                    rest(wt[:, slot, LO, :, :].rearrange("p k m -> p (k m)"), stage[:, k % RING, :],
                         wt[:, slot, HI, :, :].rearrange("p k m -> p (k m)")).then_inc(split, 1)

                def rest_lb(slot, e):
                    rows = slice(4 * RANK, 6 * RANK)
                    dve.wait_ge(lb_rounded, LB * half + e + 1)
                    rest(lbw[rows, slot, :, :], lb_raw[rows, slot, :, :], lbw[rows, slot, :, :]
                         ).then_inc(lb_split, 1)

                def rest_wd(k, n, t, tile):
                    dve.wait_ge(rounded, stage0 + n + 1)
                    rest(wd[:, t, LO, :], stage[:, k % RING, :], wd[:, t, HI, :])
                    by_part = ad[:, t, :].rearrange("p (c a b r) -> p c a b r", c=CHUNKS, a=2, b=2)
                    rest(by_part[:, :, LO, :, :],
                         ad_raw[:, :, bass.ds(tile, 1), :].rearrange("p (c b) o r -> p c b (o r)", c=CHUNKS),
                         by_part[:, :, HI, :, :]).then_inc(split, 1)

                def product(group, gate_use):
                    for chunk in range(CHUNKS):
                        dve.wait_ge(pair_free[0], freed(0, half, gate_use, chunk))
                        dve.wait_ge(groups_done, done(half, group, chunk))
                        nc.vector.tensor_tensor(tmp_p[:, chunk, :], tmp_s[:, chunk, :], pair[1][:, chunk, :],
                                                ALU.mult).then_inc(pair_free[1], 1)

                def rest_act(t, n):
                    for chunk in range(CHUNKS):
                        cols = slice(chunk * CH, (chunk + 1) * CH)
                        dve.wait_ge(act_rounded, 4 * (BLOCKS + 1) * half + 2 * n + chunk + 1)
                        rest(act[:, t, LO, cols], tmp_p[:, chunk, :], act[:, t, HI, cols]).then_inc(act_split, 1)

                def add_down(p, group, h):
                    for chunk in range(CHUNKS):
                        cols = slice(chunk * CH, (chunk + 1) * CH)
                        dve.wait_ge(groups_done, done(half, group, chunk))
                        nc.vector.tensor_tensor(resid[:, h, cols], resid[:, h, cols], pair[p][:, chunk, :],
                                                ALU.add).then_inc(pair_free[p], 1)

                def add_ldown(group):
                    for chunk in range(CHUNKS):
                        rows = slice(64 * chunk, 64 * chunk + 64)
                        dve.wait_ge(groups_done, done(half, group, chunk))
                        nc.vector.tensor_tensor(ldown[rows, :], ldown[rows, :], pair[2][rows, chunk, :],
                                                ALU.add).then_inc(pair_free[2], 1)

                def rest_x(n):
                    k = n % KT
                    dve.wait_ge(x_rounded, 2 * KT * half + n + 1)
                    rest(xs[LO][:, k, :], resid[:, k, :], xs[HI][:, k, :]).then_inc(x_split, 1)

                nc.vector.memset(ldown[:, :], 0.0).then_inc(ldown_cleared, 1)
                dve.wait_ge(rounded, stage0 + S_RANK + 1)
                rank_w = wt[:, 0, :, :, :].rearrange("p c k (a g b r) -> p c k a g b r", a=2, g=2, b=2)
                raw = stage[:, 0, :].rearrange("p (c b k g r) -> p c b k g r", c=CHUNKS, b=2, k=KT, g=2)
                for chunk in range(CHUNKS):
                    for b in range(2):
                        last = rest(rank_w[:, chunk, :, LO, :, b, :], raw[:, chunk, b, :, :, :],
                                    rank_w[:, chunk, :, HI, :, b, :])
                last.then_inc(split, 1)
                for k in range(KT):
                    rest_x(k)
                rest_wt(S_GU0, S_GU0, 1)
                for chunk in range(CHUNKS):
                    dve.wait_ge(lora_lo, 4 * half + chunk + 1)
                    dve.wait_ge(groups_done, done(half, G_RANK, chunk))
                    for b in range(2):
                        cols = slice(b * SEQ, (b + 1) * SEQ)
                        last = nc.vector.scalar_tensor_tensor(
                            out=tmp_p[0:64, chunk, cols], in0=pair[2][0:64, chunk, cols], scalar=scale_of[0:64, b:b + 1],
                            in1=tmp_s[0:64, chunk, cols], op0=ALU.mult, op1=ALU.add)
                    last.then_inc(pair_free[2], 1)
                for chunk in range(CHUNKS):
                    dve.wait_ge(lora_rounded, 4 * half + chunk + 1)
                    rest(ranks[32:64, chunk, 0, :], tmp_p[0:32, chunk, :], ranks[0:32, chunk, 0, :])
                    rest(ranks[0:32, chunk, 1, :], tmp_p[32:64, chunk, :], ranks[32:64, chunk, 1, :]
                         ).then_inc(lora_split, 1)
                rest_wt(S_GU0 + 1, S_GU0 + 1, 0)
                rest_lb(0, 0)
                rest_lb(1, 1)
                rest_wt(S_GU0 + 2, S_GU0 + 2, 1)
                rest_lb(0, 2)

                with dve.Fori(0, BLOCKS) as blk:
                    st = STAGES_BLOCK * blk
                    g = PER_BLOCK * blk + G_BLOCK
                    rest_wd(S_BLOCK, S_BLOCK + st, 0, 2 * blk)
                    product(g + G_UP_A, 2 * blk)
                    rest_act(0, 2 * blk)
                    rest_wt(S_BLOCK + 1, S_BLOCK + 1 + st, 0)
                    rest_lb(1, 4 * blk + 3)
                    rest_wt(S_BLOCK + 2, S_BLOCK + 2 + st, 1)
                    rest_lb(0, 4 * blk + 4)
                    rest_wd(S_BLOCK + 3, S_BLOCK + 3 + st, 1, 2 * blk + 1)
                    product(g + G_UP_B, 2 * blk + 1)
                    rest_act(1, 2 * blk + 1)
                    rest_wt(S_BLOCK + 4, S_BLOCK + 4 + st, 0)
                    rest_lb(1, 4 * blk + 5)
                    dve.wait_ge(ldown_cleared, half + 1)
                    dve.wait_ge(pair_free[2], free_for(2, half, 5 * blk + 1))
                    dve.wait_ge(pair_free[3], free_for(3, half, 4 * blk))
                    add_ldown(g + G_LDOWN)
                    for h in range(KT):
                        add_down(3 - h % 2, g + G_DOWN + h, h)
                        if h == 1:
                            rest_wt(S_BLOCK + 5, S_BLOCK + 5 + st, 1)
                            rest_lb(0, 4 * blk + 6)

                rest_wd(S_DOWN_LAST, S_DOWN_LAST, 0, FULL - 1)
                product(G_UP_LAST, 2 * BLOCKS)
                rest_act(0, 2 * BLOCKS)
                rest_lb(1, LB - 1)
                rest_wd(S_DOWN_TAIL, S_DOWN_TAIL, 1, FULL)
                b_down_w = wt[4 * RANK:6 * RANK, 0, :, :, :].rearrange("p c k m -> p c (k m)")
                for chunk in range(CHUNKS):
                    n = S_BDOWN + chunk
                    dve.wait_ge(rounded, stage0 + n + 1)
                    rest(b_down_w[:, chunk, :], stage[4 * RANK:6 * RANK, n % RING, :], b_down_w[:, chunk, :]
                         ).then_inc(split, 1)
                for chunk in range(CHUNKS):
                    dve.wait_ge(pair_free[0], freed(0, half, 2 * BLOCKS + 1, chunk))
                    nc.vector.tensor_tensor(tmp_p[0:TAIL, chunk, :], tmp_s[0:TAIL, chunk, :],
                                            tmp_p[0:TAIL, chunk, :], ALU.mult).then_inc(tail_product, 1)
                for chunk in range(CHUNKS):
                    cols = slice(chunk * CH, (chunk + 1) * CH)
                    dve.wait_ge(act_rounded, 4 * (BLOCKS + 1) * half + 4 * BLOCKS + 2 + chunk + 1)
                    rest(act[TAIL:2 * TAIL, 1, HI, cols], tmp_p[0:TAIL, chunk, :], act[0:TAIL, 1, HI, cols]
                         ).then_inc(act_split, 1)
                dve.wait_ge(pair_free[2], free_for(2, half, U_LDOWN_LAST))
                dve.wait_ge(pair_free[3], free_for(3, half, FIRST3[3]))
                add_ldown(G_LDOWN_LAST)
                for chunk in range(CHUNKS):
                    rows = slice(64 * chunk, 64 * chunk + 32)
                    dve.wait_ge(lora_lo, 4 * half + 2 + chunk + 1)
                    for b in range(2):
                        cols = slice(b * SEQ, (b + 1) * SEQ)
                        last = nc.vector.scalar_tensor_tensor(
                            out=tmp_p[rows, chunk, cols], in0=ldown[rows, cols], scalar=scale_of[rows, b:b + 1],
                            in1=tmp_s[rows, chunk, cols], op0=ALU.mult, op1=ALU.add)
                    last.then_inc(lora_sum, 1)
                for chunk in range(CHUNKS):
                    rows = slice(64 * chunk, 64 * chunk + 32)
                    dve.wait_ge(lora_rounded, 4 * half + 2 + chunk + 1)
                    rest(ranks[32:64, chunk, 0, :], tmp_p[rows, chunk, :], ranks[rows, chunk, 0, :]
                         ).then_inc(lora_split, 1)
                rest_wt(S_EXPERTS, S_EXPERTS, 1)
                for h in range(KT):
                    add_down(RING3[(h + 1) % 3], G_DOWN_LAST + h, h)
                    if h:
                        rest_x(KT + h - 1)
                rest_x(2 * KT - 1)
                dve.wait_ge(rounded, stage0 + S_EXPERTS_B + 1)
                rest(wd[:, 0, LO, :], stage[:, S_EXPERTS_B % RING, :], wd[:, 0, HI, :]).then_inc(split, 1)
                rest_wt(S_OUT, S_OUT, 0)
                rest_wt(S_OUT + 1, S_OUT + 1, 1)

                def link(instruction, step):
                    instruction.then_inc(route_step, 1)
                    if step < ROUTE_STEPS:
                        dve.wait_ge(route_step, ROUTE_STEPS * half + step)

                def over(ap, n):
                    return ap.unsqueeze(ap.ndim).to_broadcast(list(ap.shape) + [n])

                dve.wait_ge(bias_ready, 1)
                dve.wait_ge(pair_free[0], freed(0, half, 2 * BLOCKS + 3))
                link(nc.vector.tensor_tensor(logits[:, :, :], logits2[:, :, HI, :], logits2[:, :, LO, :], ALU.add), 1)
                for t in range(TT // SEQ_HALF):
                    by_seq = logits[:, :, :].rearrange("p (s t) e -> p s t e", t=TT // SEQ_HALF)[:, :, t, :]
                    last = nc.vector.tensor_tensor(by_seq, by_seq, lang_bias[:, bass.ds(SEQ_HALF * half, SEQ_HALF), :],
                                                   ALU.add)
                link(last, 2)
                nc.vector.tensor_reduce(highest[:, :], logits[:, :, :], mybir.AxisListType.X, ALU.max)
                for t in range(TT):
                    last = nc.vector.max(best[:, t, :], logits[:, t, :])
                link(last, 3)
                nc.vector.tensor_tensor(odds[:, 0, :], best[:, :, 1], highest[:, :], ALU.subtract
                                        ).then_inc(route_step, 1)
                for t in range(TT):
                    last = nc.vector.max_index(best_at[:, t, :], best[:, t, :], logits[:, t, :])
                link(last, 5)
                nc.vector.tensor_copy(best_no[:, :, :], best_at[:, :, 0:2])
                dve.wait_ge(exp_ready, half + 1)
                link(nc.vector.tensor_scalar(weight[:, 0, :], odds[:, 1, :], 1.0, None, ALU.add), 6)
                link(nc.vector.reciprocal(weight[:, 1, :], weight[:, 0, :]), 7)
                link(nc.vector.tensor_scalar(weight[:, 2, :], weight[:, 1, :], SCALING, None, ALU.mult), 8)
                nc.vector.tensor_tensor(weight[:, 3, :], weight[:, 2, :], odds[:, 1, :], ALU.mult)
                numbers = expert[:, :].unsqueeze(1).to_broadcast([P, TT, EXPERTS])
                for i in range(2):
                    last = nc.vector.tensor_tensor(picked[:, i, :, :], numbers, over(best_no[:, :, i], EXPERTS),
                                                   ALU.is_equal)
                link(last, 9)
                for i in range(2):
                    last = nc.vector.tensor_tensor(picked[:, i, :, :], picked[:, i, :, :],
                                                   over(weight[:, 2 + i, :], EXPERTS), ALU.mult)
                link(last, 10)
                by_token = picked[:, :, :, :].rearrange("p i t e -> p i (t e)")
                link(nc.vector.tensor_tensor(
                    tmp_p[:, :, :].rearrange("p c n -> p (c n)").rearrange("p (n r) -> p n r", r=RANK),
                    over(by_token[:, 0, :], RANK), over(by_token[:, 1, :], RANK), ALU.add), 11)

                for chunk in range(CHUNKS):
                    dve.wait_ge(pair_free[0], freed(0, half, 2 * BLOCKS + 4, chunk))
                    nc.vector.tensor_tensor(tmp_p[:, chunk, :], tmp_s[:, chunk, :], pair[1][:, chunk, :],
                                            ALU.mult).then_inc(pair_free[1], 1)
                for chunk in range(CHUNKS):
                    cols = slice(chunk * CH, (chunk + 1) * CH)
                    dve.wait_ge(hg_rounded, 2 * half + chunk + 1)
                    rest(act[:, 0, LO, cols], tmp_p[:, chunk, :], act[:, 0, HI, cols]).then_inc(hg_split, 1)
                rest_wt(S_OUT + 2, S_OUT + 2, 0)
                for o in range(KT):
                    if o + 3 < KT:
                        rest_wt(S_OUT + o + 3, S_OUT + o + 3, (o + 3) % 2)
                    add_down(RING3[o % 3], G_OUT + o, o)


_OUT = (HALVES, KT, P, NT)


def kernel(**inputs):
    import numpy as np
    import concourse.bacc as bacc
    from concourse.bass_utils import run_bass_kernel_spmd

    v = {name: np.asarray(a) for name, a in inputs.items()}

    def width_tiles(w):
        return np.ascontiguousarray(w.reshape(-1, P, KT, P).transpose(0, 3, 2, 1)).reshape(-1, P, D)

    gate, up = v["L0_cond_W_gate"], v["L0_cond_W_up"]
    full = FULL * P
    pairs = np.stack([gate[:full].reshape(FULL, P, D), up[:full].reshape(FULL, P, D)], 1).reshape(-1, D)
    w_gu = width_tiles(np.concatenate([pairs, gate[full:], up[full:]]))
    down_t = v["L0_cond_W_down"].T
    w_down = np.concatenate([down_t, down_t[full:]]).reshape(FT, P, D)
    a_g, a_u = v["L0_cond_A_gate"][0], v["L0_cond_A_up"][0]
    a_gu = np.stack([a_g, a_u], 1).reshape(ADAPTERS, 2, RANK, KT, P).transpose(0, 4, 3, 1, 2).reshape(ADAPTERS, P, -1)
    b_g, b_u = (v[n][0].transpose(0, 2, 1) for n in ("L0_cond_B_gate", "L0_cond_B_up"))
    b_gu = np.zeros((ADAPTERS, RANK, LB, P), b_g.dtype)
    b_gu[:, :, 0:2 * FULL:2] = b_g[:, :, :full].reshape(ADAPTERS, RANK, FULL, P)
    b_gu[:, :, 1:2 * FULL:2] = b_u[:, :, :full].reshape(ADAPTERS, RANK, FULL, P)
    b_gu[:, :, LB - 2, :TAIL] = b_g[:, :, full:]
    b_gu[:, :, LB - 1, TAIL:] = b_u[:, :, full:]
    a_d = v["L0_cond_A_down"][0]
    a_down = np.concatenate([a_d, a_d[:, :, full:]], 2).reshape(ADAPTERS, RANK, FT, P)
    a_down = a_down.transpose(0, 3, 2, 1).reshape(ADAPTERS, P, FT * RANK)
    tokens = v["x"].reshape(HALVES, NT, KT, P)
    rows = np.arange(P)
    arrays = {
        "x_t": tokens.transpose(0, 2, 3, 1),
        "w_gu": w_gu,
        "w_down": w_down,
        "a_gu": a_gu,
        "b_gu": b_gu,
        "a_down": a_down,
        "b_down": v["L0_cond_B_down"][0].transpose(0, 2, 1),
        "w_out": width_tiles(v["L1_cond_W"]),
        "a_exp": width_tiles(v["L1_cond_A"].reshape(EXPERTS * RANK, D))[0],
        "b_exp": v["L1_cond_B"].transpose(0, 2, 1).reshape(EXPERTS * RANK, D),
        "w_route": v["L1_cond_Wr"].reshape(EXPERTS, KT, P).transpose(2, 1, 0),
        "adapter_of": v["itok_B_2_6"].reshape(1, NSEQ),
        "language_of": v["itok_B_0_7"].reshape(1, NSEQ),
        "identity": np.eye(P, dtype=np.float32),
        "seq_scale": np.stack([np.where(rows // RANK % 2 == b, LORA_SCALE, 0.0) for b in range(2)], 1).astype(np.float32),
        "expert_no": np.tile(np.arange(EXPERTS, dtype=np.float32), (P, 1)),
    }
    arrays = {name: np.ascontiguousarray(a) for name, a in arrays.items()}
    nc = bacc.Bacc("TRN2", target_bir_lowering=False, num_devices=1)
    args = [nc.dram_tensor(n, a.shape, mybir.dt.from_np(a.dtype), kind="ExternalInput").ap() for n, a in arrays.items()]
    args.append(nc.dram_tensor("out", _OUT, F32, kind="ExternalOutput").ap())
    cond_resid_kernel(nc, *args)
    got = run_bass_kernel_spmd(nc, [arrays], core_ids=[0]).results[0]["out"]
    return np.ascontiguousarray(got.transpose(0, 3, 1, 2)).reshape(NSEQ, SEQ, D)
```

```python
from contextlib import ExitStack

import concourse.bass as bass
from concourse import mybir

P = 128
D = 1024
F = 2752
KT = D // P
FULL = F // P
TAIL = F - FULL * P
FT = FULL + 1
SEQ = 256
NSEQ = 8
HALVES = 2
SEQ_HALF = NSEQ // HALVES
CHUNKS = 2
CH = 2 * SEQ
NT = CHUNKS * CH
RANK = 16
ADAPTERS = 16
EXPERTS = 8
LANG_BIAS = 5.0
SCALING = 2.0
LORA_SCALE = 0.5
GU = 2 * FULL + 1
LB = GU + 1
BLOCKS = (FULL - 1) // 2

G_RANK, G_GATE0, G_BLOCK, PER_BLOCK = 0, 1, 2, 13
G_UP_A, G_GATE_B, G_UP_B, G_GATE_NEXT, G_LDOWN, G_DOWN = 0, 1, 2, 3, 4, 5
G_UP_LAST = G_BLOCK + PER_BLOCK * BLOCKS
G_TAIL = G_UP_LAST + 1
G_LDOWN_LAST = G_TAIL + 1
G_DOWN_LAST = G_LDOWN_LAST + 1
G_ROUTER = G_DOWN_LAST + KT
G_EXPERTS = G_ROUTER + 1
G_LOGITS_T = G_EXPERTS + 1
G_GATES_T = G_LOGITS_T + 1
G_OUT = G_GATES_T + 1
GROUPS = G_OUT + KT

S_RANK, S_GU0, S_BLOCK, STAGES_BLOCK = 0, 1, 4, 6
S_DOWN_LAST = S_BLOCK + STAGES_BLOCK * BLOCKS
S_DOWN_TAIL = S_DOWN_LAST + 1
S_BDOWN = S_DOWN_TAIL + 1
S_EXPERTS = S_BDOWN + 2
S_EXPERTS_B = S_EXPERTS + 1
S_OUT = S_EXPERTS_B + 1
STAGES = S_OUT + KT
RING = 3
LOADED = 96
assert STAGES % RING == 0 and LB % 2 == 0

USES = (2 * BLOCKS + 6, 2 * BLOCKS + 6, 5 * BLOCKS + 7, 4 * BLOCKS + 6)
RING4 = (2, 3, 1, 0)
FIRST4 = {2: 5 * BLOCKS + 1, 3: 4 * BLOCKS, 1: 2 * BLOCKS + 1, 0: 2 * BLOCKS + 2}
RING3 = (2, 3, 1)
FIRST3 = {2: 5 * BLOCKS + 4, 3: 4 * BLOCKS + 3, 1: 2 * BLOCKS + 4}
U_TAIL = 2 * BLOCKS + 1
U_ROUTER = 4 * BLOCKS + 2
U_EXPERTS = 2 * BLOCKS + 3
U_LOGITS_T = 2 * BLOCKS + 4
U_GATES_T = 2 * BLOCKS + 5


def last_block(j):
    p = RING4[j % 4]
    return p, FIRST4[p] + j // 4


def out_tile(o):
    p = RING3[o % 3]
    return p, FIRST3[p] + o // 3


ROUTE_STEPS = 11

ALU = mybir.AluOpType
ACT = mybir.ActivationFunctionType
F32 = mybir.dt.float32
F32R = mybir.dt.float32r
I32 = mybir.dt.int32
U32 = mybir.dt.uint32

HI, LO = 0, 1
PASSES = ((HI, HI), (HI, LO), (LO, HI))
RANK_PASSES = (HI, LO)


def cond_resid_kernel(nc, x_t, w_gu, w_down, a_gu, b_gu, a_down, b_down, w_out, a_exp, b_exp, w_route,
                      adapter_of, language_of, identity, seq_scale, expert_no, out):
    with ExitStack() as ctx:
        def sb(name, shape, dt=F32):
            return ctx.enter_context(nc.sbuf_tensor(name, shape, dt))

        def sem(name):
            return ctx.enter_context(nc.semaphore(name))

        lb_dram = nc.dram_tensor("lb_dram", (HALVES, LB, 2 * RANK, CHUNKS, P), F32).ap()

        xs = [sb("x_hi", [P, KT, NT], F32R), sb("x_lo", [P, KT, NT], F32R)]
        resid = sb("resid", [P, KT, NT])
        act = sb("act", [P, 2, 2, NT], F32R)
        wd = sb("wd", [P, 2, 2, D], F32R)
        ad = sb("ad", [P, 2, P], F32R)
        wt = sb("wt", [P, 2, 2, KT, P], F32R)
        stage = sb("stage", [P, RING, D])
        lb_raw = sb("lb_raw", [3 * 2 * RANK, 2, CHUNKS, P])
        lbw = sb("lbw", [3 * 2 * RANK, 2, CHUNKS, P], F32R)
        ranks = sb("ranks", [3 * 2 * RANK, CHUNKS, 2, CH], F32R)
        ldown = sb("ldown", [P, CH])
        ad_raw = sb("ad_raw", [P, SEQ_HALF, FT, RANK])
        tmp_s = sb("tmp_s", [P, CHUNKS, CH])
        tmp_p = sb("tmp_p", [P, CHUNKS, CH])
        route_raw = sb("route_raw", [P, KT, EXPERTS])
        route_w = sb("route_w", [P, KT, 2, EXPERTS], F32R)
        ident = sb("ident", [P, P])
        scale_of = sb("scale_of", [P, 2])
        expert = sb("expert", [P, EXPERTS])
        adapters = sb("adapters", [1, NSEQ], I32)
        lang_i = sb("lang_i", [P, NSEQ], I32)
        lang = sb("lang", [P, NSEQ])
        lang_bias = sb("lang_bias", [P, NSEQ, EXPERTS])
        TT = NT // P
        logits2 = sb("logits2", [P, TT, 2, EXPERTS])
        logits = sb("logits", [P, TT, EXPERTS])
        best = sb("best", [P, TT, 8])
        best_at = sb("best_at", [P, TT, 8], U32)
        best_no = sb("best_no", [P, TT, 2])
        highest = sb("highest", [P, TT])
        odds = sb("odds", [P, 2, TT])
        weight = sb("weight", [P, 4, TT])
        picked = sb("picked", [P, 2, TT, EXPERTS])

        pair = [ctx.enter_context(nc.psum_tensor(f"pair{i}", [P, CHUNKS, CH], F32)) for i in range(4)]

        const_in = sem("const_in")
        adapters_in = sem("adapters_in")
        lb_gathered = sem("lb_gathered")
        stage_in = [sem(f"stage_in{i}") for i in range(RING)]
        lb_in = [sem(f"lb_in{i}") for i in range(2)]
        ad_in = sem("ad_in")
        x_in = [sem(f"x_in{k}") for k in range(KT)]
        out_stored = [sem(f"out_stored{k}") for k in range(KT)]
        rounded = sem("rounded")
        split = sem("split")
        lb_rounded = sem("lb_rounded")
        lb_split = sem("lb_split")
        gate0_rounded = sem("gate0_rounded")
        xs_free = sem("xs_free")
        x_rounded = sem("x_rounded")
        x_split = sem("x_split")
        groups_done = sem("groups_done")
        pair_free = [sem(f"pair_free{i}") for i in range(4)]
        act_rounded = sem("act_rounded")
        act_split = sem("act_split")
        tail_product = sem("tail_product")
        ldown_cleared = sem("ldown_cleared")
        lora_lo = sem("lora_lo")
        lora_sum = sem("lora_sum")
        lora_rounded = sem("lora_rounded")
        lora_up_rounded = sem("lora_up_rounded")
        lora_split = sem("lora_split")
        route_rounded = sem("route_rounded")
        route_ready = sem("route_ready")
        lang_ready = sem("lang_ready")
        bias_ready = sem("bias_ready")
        route_step = sem("route_step")
        exp_ready = sem("exp_ready")
        hg_rounded = sem("hg_rounded")
        hg_split = sem("hg_split")

        def done(half, group, chunk=1):
            return 2 * GROUPS * half + (2 * GROUPS + 2 * group + chunk + 1)

        def done_last_half(half, group):
            return 2 * GROUPS * half + (2 * group + 2)

        def freed(p, half, use, chunk=1):
            return 2 * USES[p] * half + 2 * use + (chunk + 3)

        def free_for(p, half, use, chunk=1):
            return 2 * USES[p] * half + 2 * use + (chunk + 1)

        block = ctx.enter_context(nc.Block())

        @block.gpsimd
        def _(pool):
            def load_x(half, k):
                if half:
                    pool.wait_ge(out_stored[k], 16 * half)
                pool.dma_start(resid[:, k, :], x_t[half, k]).then_inc(x_in[k], 16)

            def gather_lb(half):
                for s in range(SEQ_HALF):
                    chunk, b = divmod(s, 2)
                    n = half * SEQ_HALF + s
                    a = pool.value_load(adapters[0:1, n:n + 1], min_val=0, max_val=ADAPTERS - 1)
                    src = b_gu[bass.ds(a, 1)].rearrange("o r t f -> (o r) t f")
                    dst = lb_dram[half, :, b * RANK:(b + 1) * RANK, chunk, :].rearrange("t r f -> r t f")
                    pool.dma_start(dst, src).then_inc(lb_gathered, 16)
                pool.wait_ge(lb_gathered, 16 * SEQ_HALF * (half + 1))

            def store_out(half, o):
                p, use = out_tile(o)
                pool.wait_ge(pair_free[p], freed(p, half, use))
                pool.dma_start(out[half, o], resid[:, o, :]).then_inc(out_stored[o], 16)

            for k in range(KT):
                load_x(0, k)
            pool.wait_ge(adapters_in, 16)
            pool.wait_ge(x_in[KT // 2], 16)
            gather_lb(0)
            gather_lb(1)
            for o in range(KT):
                store_out(0, o)
                if o >= 2:
                    load_x(1, o - 2)
            load_x(1, KT - 2)
            load_x(1, KT - 1)
            for o in range(KT):
                store_out(1, o)
            for k in range(KT):
                pool.wait_ge(out_stored[k], 16 * HALVES)

        @block.sync
        def _(sp):
            sp.dma_start(adapters[:, :], adapter_of).then_inc(adapters_in, 16)
            sp.wait_ge(adapters_in, 16)
            with sp.Fori(0, HALVES) as half:
                stage0 = STAGES * half

                def slot_free(n):
                    sp.wait_ge(split, n + 1)

                def adapter(s):
                    return sp.value_load(adapters[0:1, bass.ds(SEQ_HALF * half + s, 1)],
                                         min_val=0, max_val=ADAPTERS - 1)

                def load(k, base, src):
                    slot_free(base + k)
                    sp.dma_start(stage[:, k % RING, :], src).then_inc(stage_in[k % RING], LOADED)

                def load_lb(e):
                    sp.wait_ge(lb_split, LB * half + e + 1)
                    return e

                def lb_dmas(slot, e):
                    for part in range(3):
                        rows = slice(part * 2 * RANK, (part + 1) * 2 * RANK)
                        sp.dma_start(lb_raw[rows, slot, :, :],
                                     lb_dram[bass.ds(half, 1), bass.ds(e, 1)].rearrange("a b r c f -> (a b r) c f")
                                     ).then_inc(lb_in[slot], 16)

                def one(t, n):
                    return t[bass.ds(n, 1)].rearrange("o p n -> (o p) n")

                of = [adapter(s) for s in range(SEQ_HALF)]
                load(S_GU0, stage0, w_gu[0])
                slot_free(stage0)
                for s in range(SEQ_HALF):
                    sp.dma_start(stage[:, 0, s * 256:(s + 1) * 256], one(a_gu, of[s])
                                 ).then_inc(stage_in[0], 32 if s % 2 else 16)
                for s in range(SEQ_HALF):
                    sp.dma_start(ad_raw[:, s, :, :].rearrange("p t r -> p (t r)"), one(a_down, of[s])
                                 ).then_inc(ad_in, 16)
                load(S_GU0 + 1, stage0, w_gu[1])
                sp.wait_ge(lb_gathered, 16 * SEQ_HALF * half + 16 * SEQ_HALF)
                for e in range(3):
                    load_lb(e)
                    lb_dmas(e % 2, e)
                    if e == 0:
                        load(S_GU0 + 2, stage0, w_gu[2])

                with sp.Fori(0, BLOCKS) as blk:
                    base = stage0 + STAGES_BLOCK * blk
                    tile = 4 * blk
                    load(S_BLOCK + 0, base, one(w_down, 2 * blk))
                    load(S_BLOCK + 1, base, one(w_gu, tile + 3))
                    load_lb(tile + 3)
                    lb_dmas(1, tile + 3)
                    load(S_BLOCK + 2, base, one(w_gu, tile + 4))
                    load_lb(tile + 4)
                    lb_dmas(0, tile + 4)
                    load(S_BLOCK + 3, base, one(w_down, 2 * blk + 1))
                    load(S_BLOCK + 4, base, one(w_gu, tile + 5))
                    load_lb(tile + 5)
                    lb_dmas(1, tile + 5)
                    load(S_BLOCK + 5, base, one(w_gu, tile + 6))
                    load_lb(tile + 6)
                    lb_dmas(0, tile + 6)

                load(S_DOWN_LAST, stage0, w_down[FULL - 1])
                load_lb(LB - 1)
                lb_dmas(1, LB - 1)
                load(S_DOWN_TAIL, stage0, w_down[FULL])
                for chunk in range(CHUNKS):
                    n = S_BDOWN + chunk
                    slot_free(stage0 + n)
                    for b in range(2):
                        for part in range(3):
                            row = part * 2 * RANK + b * RANK
                            sp.dma_start(stage[row:row + RANK, n % RING, :], one(b_down, of[2 * chunk + b])
                                         ).then_inc(stage_in[n % RING], 16)
                load(S_EXPERTS, stage0, a_exp)
                load(S_EXPERTS_B, stage0, b_exp)
                for o in range(KT):
                    load(S_OUT + o, stage0, w_out[o])

        @block.tensor
        def _(pe):
            pe.sem_inc(groups_done, 2 * GROUPS)
            pe.sem_inc(xs_free, KT)
            with pe.Fori(0, HALVES) as half:

                def stages_ready(n):
                    pe.wait_ge(split, STAGES * half + n + (RING + 1))

                def banks_free(p, use):
                    pe.wait_ge(pair_free[p], free_for(p, half, use))

                def columns(chunk):
                    return slice(chunk * CH, (chunk + 1) * CH)

                def width_pass(p, slot, k, w, a, start=False, stop=False):
                    for chunk in range(CHUNKS):
                        mm = nc.tensor.matmul(pair[p][:, chunk, :], wt[:, slot, w, k, :], xs[a][:, k, columns(chunk)],
                                              start=start, stop=stop)
                        if stop:
                            mm.then_inc(groups_done, 1)
                    return mm

                def width_product(p, use, slot, stop, also_wait=None, last_read=False):
                    banks_free(p, use)
                    for k in range(KT):
                        if also_wait and k == KT // 2:
                            also_wait()
                        for w, a in PASSES:
                            mm = width_pass(p, slot, k, w, a, start=(k == 0 and (w, a) == (HI, HI)),
                                            stop=(stop and k == KT - 1 and w == LO))
                        if last_read:
                            mm.then_inc(xs_free, 1)

                def lora_tile(p, e, slot, side, last=True):
                    pe.wait_ge(lb_split, LB * half + e + 3)
                    for chunk in range(CHUNKS):
                        mm = nc.tensor.matmul(pair[p][:, chunk, :], lbw[:, slot, chunk, :],
                                              ranks[:, chunk, side, :], start=False, stop=last)
                        if last:
                            mm.then_inc(groups_done, 1)

                def gate_or_up(p, use, n, e, side):
                    stages_ready(n)
                    width_product(p, use, 1 - side, stop=False)
                    lora_tile(p, e, side, side)

                def down_product(p, h, t, tail, stop):
                    if not tail:
                        parts = [(wd[:, t, w, h * P:(h + 1) * P], act[:, t, a]) for w, a in PASSES]
                    else:
                        parts = [(wd[:, t, HI, h * P:(h + 1) * P], act[:, t, HI]),
                                 (wd[0:TAIL, t, LO, h * P:(h + 1) * P], act[0:TAIL, t, HI])]
                    for i, (weights, values) in enumerate(parts):
                        for chunk in range(CHUNKS):
                            last = stop and i == len(parts) - 1
                            mm = nc.tensor.matmul(pair[p][:, chunk, :], weights, values[:, columns(chunk)],
                                                  start=(t == 0 and i == 0), stop=last)
                            if last:
                                mm.then_inc(groups_done, 1)

                def lora_down(p, t, tail):
                    for a in RANK_PASSES[:1 if tail else 2]:
                        for chunk in range(CHUNKS):
                            last = t == 1 and (tail or a == LO)
                            mm = nc.tensor.matmul(pair[p][:, chunk, :], ad[:, t, :], act[:, t, a, columns(chunk)],
                                                  start=(t == 0 and a == HI), stop=last)
                            if last:
                                mm.then_inc(groups_done, 1)

                rank_w = wt[:, 0, :, :, :].rearrange("p c k m -> p (c k) m")

                def rank_pass(k, a):
                    for chunk in range(CHUNKS):
                        mm = nc.tensor.matmul(pair[2][:, chunk, :], rank_w[:, chunk * KT + k, :],
                                              xs[a][:, k, columns(chunk)],
                                              start=(k == 0 and a == HI), stop=(k == KT - 1 and a == LO))
                        if k == KT - 1 and a == LO:
                            mm.then_inc(groups_done, 1)

                pe.wait_ge(gate0_rounded, half + 1)
                banks_free(0, 0)
                for k in range(KT + KT // 2):
                    if k < KT:
                        pe.wait_ge(x_rounded, 2 * KT * half + k + 1)
                        width_pass(0, 1, k, HI, HI, start=(k == 0))
                    if k == KT // 2:
                        stages_ready(S_RANK)
                        banks_free(2, 0)
                    if k >= KT // 2:
                        rank_pass(k - KT // 2, HI)
                for k in range(KT):
                    pe.wait_ge(x_split, 2 * KT * half + k + 1)
                    rank_pass(k, LO)
                for k in range(KT):
                    width_pass(0, 1, k, HI, LO)
                stages_ready(S_GU0)
                for k in range(KT):
                    width_pass(0, 1, k, LO, HI)
                pe.wait_ge(lora_split, 4 * half + 2)
                lora_tile(0, 0, 0, 0)

                with pe.Fori(0, BLOCKS) as blk:
                    st = STAGES_BLOCK * blk
                    gate_or_up(1, 2 * blk, S_GU0 + 1 + st, 4 * blk + 1, 1)
                    gate_or_up(0, 2 * blk + 1, S_GU0 + 2 + st, 4 * blk + 2, 0)
                    gate_or_up(1, 2 * blk + 1, S_BLOCK + 1 + st, 4 * blk + 3, 1)
                    gate_or_up(0, 2 * blk + 2, S_BLOCK + 2 + st, 4 * blk + 4, 0)
                    stages_ready(S_BLOCK + 3 + st)
                    pe.wait_ge(act_split, 4 * (BLOCKS + 1) * half + 4 * blk + 4)
                    for g in range(1 + KT):
                        p, use = (2, 5 * blk + 1 + g // 2) if g % 2 == 0 else (3, 4 * blk + g // 2)
                        banks_free(p, use)
                        for t in range(2):
                            if g == 0:
                                lora_down(p, t, tail=False)
                            else:
                                down_product(p, g - 1, t, tail=False, stop=(t == 1))

                gate_or_up(1, 2 * BLOCKS, S_DOWN_LAST - 2, LB - 3, 1)
                stages_ready(S_DOWN_LAST - 1)
                width_product(0, U_TAIL, 1, stop=False)
                lora_tile(0, LB - 2, 0, 0, last=False)
                lora_tile(0, LB - 1, 1, 1)
                b_down_w = wt[0:3 * 2 * RANK, 0, :, :, :].rearrange("p c k m -> p c (k m)")

                def last_first(j):
                    p, use = last_block(j)
                    banks_free(p, use)
                    if j == 0:
                        lora_down(p, 0, tail=False)
                    else:
                        down_product(p, j - 1, 0, tail=False, stop=False)

                def last_second(j):
                    p, _ = last_block(j)
                    if j == 0:
                        lora_down(p, 1, tail=True)
                    else:
                        down_product(p, j - 1, 1, tail=True, stop=False)

                def last_lora(j):
                    p, _ = last_block(j)
                    for chunk in range(CHUNKS):
                        nc.tensor.matmul(pair[p][:, chunk, :], b_down_w[:, chunk, (j - 1) * P:j * P],
                                         ranks[:, chunk, 0, :], start=False, stop=True).then_inc(groups_done, 1)

                stages_ready(S_DOWN_LAST)
                pe.wait_ge(act_split, 4 * (BLOCKS + 1) * half + 4 * BLOCKS + 2)
                for j in range(4):
                    last_first(j)
                stages_ready(S_DOWN_TAIL)
                pe.wait_ge(act_split, 4 * (BLOCKS + 1) * half + 4 * BLOCKS + 4)
                for j in range(4):
                    last_second(j)
                last_first(4)
                last_second(4)
                stages_ready(S_BDOWN + 1)
                pe.wait_ge(lora_split, 4 * half + 4)
                last_lora(1)
                for j in range(5, KT + 1):
                    last_lora(j - 3)
                    last_first(j)
                    last_second(j)
                for j in range(KT - 2, KT + 1):
                    last_lora(j)

                pe.wait_ge(route_ready, 1)
                banks_free(3, U_ROUTER)
                for k in range(KT):
                    pe.wait_ge(x_split, 2 * KT * half + KT + k + 1)
                    for a in RANK_PASSES:
                        for chunk in range(CHUNKS):
                            last = k == KT - 1 and a == LO
                            mm = nc.tensor.matmul(pair[3][0:2 * EXPERTS, chunk, :],
                                                  route_w[:, k, :, :].rearrange("p a e -> p (a e)"),
                                                  xs[a][:, k, columns(chunk)],
                                                  start=(k == 0 and a == HI), stop=last)
                            if last:
                                mm.then_inc(groups_done, 1)
                stages_ready(S_EXPERTS)

                def before_transposes():
                    pe.wait_ge(pair_free[3], freed(3, half, U_ROUTER))
                    banks_free(0, U_LOGITS_T)

                width_product(1, U_EXPERTS, 1, stop=True, also_wait=before_transposes)
                per_chunk = TT // CHUNKS
                for chunk in range(CHUNKS):
                    for t in range(per_chunk):
                        mm = nc.tensor.transpose(pair[0][:, chunk, t * 2 * EXPERTS:(t + 1) * 2 * EXPERTS],
                                                 tmp_s[0:2 * EXPERTS, chunk, t * P:(t + 1) * P],
                                                 ident[0:2 * EXPERTS, 0:2 * EXPERTS])
                    mm.then_inc(groups_done, 1)

                def out_main(o):
                    p, use = out_tile(o)
                    stages_ready(S_OUT + o)
                    width_product(p, use, o % 2, stop=False, last_read=(o == KT - 1))

                def out_lora(o):
                    p, _ = out_tile(o)
                    if o == 0:
                        pe.wait_ge(hg_split, 2 * half + 2)
                    for w, a in PASSES:
                        for chunk in range(CHUNKS):
                            mm = nc.tensor.matmul(pair[p][:, chunk, :], wd[:, 0, w, o * P:(o + 1) * P],
                                                  act[:, 0, a, columns(chunk)], start=False, stop=(w == LO))
                            if w == LO:
                                mm.then_inc(groups_done, 1)

                out_main(0)
                pe.wait_ge(route_step, ROUTE_STEPS * half + ROUTE_STEPS)
                banks_free(0, U_GATES_T)
                for chunk in range(CHUNKS):
                    for t in range(per_chunk):
                        mm = nc.tensor.transpose(pair[0][:, chunk, t * P:(t + 1) * P],
                                                 tmp_p[:, chunk, t * P:(t + 1) * P], ident[:, :])
                    mm.then_inc(groups_done, 1)
                for o in range(1, KT):
                    out_main(o)
                    out_lora(o - 1)
                out_lora(KT - 1)

        @block.scalar
        def _(sc):
            def copy(dst, src, **kw):
                return nc.scalar.activation(dst, src, ACT.Copy, **kw)

            sc.sem_inc(pair_free[0], 2)
            sc.dma_start(scale_of[:, :], seq_scale).then_inc(const_in, 16)
            sc.dma_start(route_raw[:, :, :], w_route).then_inc(const_in, 16)
            sc.dma_start(lang_i[:, :], language_of.to_broadcast([P, NSEQ])).then_inc(const_in, 16)
            sc.dma_start(expert[:, :], expert_no).then_inc(const_in, 16)
            sc.dma_start(ident[:, :], identity).then_inc(const_in, 16)
            sc.wait_ge(const_in, 16 * 5)
            copy(route_w[:, :, HI, :], route_raw[:, :, :]).then_inc(route_rounded, 1)
            with sc.Fori(0, HALVES) as half:
                stage0 = STAGES * half

                def arrived(k, base):
                    h, blk = base
                    sc.wait_ge(stage_in[k % RING],
                               LOADED * (STAGES // RING) * h + LOADED * (STAGES_BLOCK // RING) * blk
                               + LOADED * (k // RING + 1))

                def round_wt(k, blk, slot, free_at):
                    sc.wait_ge(groups_done, free_at)
                    arrived(k, (half, blk))
                    copy(wt[:, slot, HI, :, :].rearrange("p k m -> p (k m)"), stage[:, k % RING, :]
                         ).then_inc(rounded, 1)

                def round_lb(slot, e, in_count):
                    sc.wait_ge(lb_in[slot], in_count)
                    copy(lbw[:, slot, :, :], lb_raw[:, slot, :, :]).then_inc(lb_rounded, 1)

                def lb_count(e_half, blk=0):
                    return 48 * (LB // 2) * half + 48 * 2 * blk + 48 * (e_half // 2 + 1)

                def round_wd(k, blk, t, free_at, tile):
                    sc.wait_ge(groups_done, free_at)
                    arrived(k, (half, blk))
                    copy(wd[:, t, HI, :], stage[:, k % RING, :])
                    sc.wait_ge(ad_in, 64 * half + 64)
                    copy(ad[:, t, :].rearrange("p (c a b r) -> p c a b r", c=CHUNKS, a=2, b=2)[:, :, HI, :, :],
                         ad_raw[:, :, bass.ds(tile, 1), :].rearrange("p (c b) o r -> p c b (o r)", c=CHUNKS)
                         ).then_inc(rounded, 1)

                def silu(group, use, s_free):
                    for chunk in range(CHUNKS):
                        sc.wait_ge(groups_done, done(half, group, chunk))
                        sc.wait_ge(pair_free[1], free_for(1, half, s_free, chunk))
                        nc.scalar.activation(tmp_s[:, chunk, :], pair[0][:, chunk, :], ACT.Silu
                                             ).then_inc(pair_free[0], 1)

                def round_act(t, up_use):
                    for chunk in range(CHUNKS):
                        sc.wait_ge(pair_free[1], freed(1, half, up_use, chunk))
                        copy(act[:, t, HI, chunk * CH:(chunk + 1) * CH], tmp_p[:, chunk, :]
                             ).then_inc(act_rounded, 1)

                def round_x(k):
                    sc.wait_ge(xs_free, KT * half + k + 1)
                    sc.wait_ge(x_in[k], 16 * half + 16)
                    copy(xs[HI][:, k, :], resid[:, k, :]).then_inc(x_rounded, 1)

                for k in range(KT // 2):
                    round_x(k)
                sc.wait_ge(groups_done, done_last_half(half, G_GATES_T + KT - 2))
                arrived(S_RANK, (half, 0))
                rank_w = wt[:, 0, :, :, :].rearrange("p c k (a g b r) -> p c k a g b r", a=2, g=2, b=2)
                raw = stage[:, 0, :].rearrange("p (c b k g r) -> p c b k g r", c=CHUNKS, b=2, k=KT, g=2)
                for chunk in range(CHUNKS):
                    for b in range(2):
                        last = copy(rank_w[:, chunk, :, HI, :, b, :], raw[:, chunk, b, :, :, :])
                last.then_inc(rounded, 1)
                for k in range(KT // 2, KT):
                    round_x(k)
                for chunk in range(CHUNKS):
                    sc.wait_ge(groups_done, done(half, G_RANK, chunk))
                    for b in range(2):
                        cols = slice(b * SEQ, (b + 1) * SEQ)
                        last = copy(tmp_s[0:64, chunk, cols], pair[2][64:128, chunk, cols],
                                    scale=scale_of[64:128, b:b + 1])
                    last.then_inc(lora_lo, 1)
                for chunk in range(CHUNKS):
                    sc.wait_ge(pair_free[2], freed(2, half, 0, chunk))
                    copy(ranks[0:32, chunk, 0, :], tmp_p[0:32, chunk, :]).then_inc(lora_rounded, 1)
                    copy(ranks[64:96, chunk, 0, :], tmp_p[0:32, chunk, :]).then_inc(lora_rounded, 1)
                round_wt(S_GU0 + 1, 0, 0, done(half, G_RANK))
                round_lb(0, 0, lb_count(0))
                round_lb(1, 1, lb_count(1))
                silu(G_GATE0, 0, 0)
                round_wt(S_GU0 + 2, 0, 1, done(half, G_GATE0))
                round_lb(0, 2, lb_count(2))

                with sc.Fori(0, BLOCKS) as blk:
                    g = PER_BLOCK * blk + G_BLOCK
                    round_wd(S_BLOCK, blk, 0, done(half, g - 1), 2 * blk)
                    round_act(0, 2 * blk)
                    round_wt(S_BLOCK + 1, blk, 0, done(half, g + G_UP_A))
                    round_lb(1, 3, lb_count(3, blk))
                    silu(g + G_GATE_B, 2 * blk + 1, 2 * blk + 1)
                    round_wt(S_BLOCK + 2, blk, 1, done(half, g + G_GATE_B))
                    round_lb(0, 4, lb_count(4, blk))
                    round_wd(S_BLOCK + 3, blk, 1, done(half, g - 1), 2 * blk + 1)
                    round_act(1, 2 * blk + 1)
                    round_wt(S_BLOCK + 4, blk, 0, done(half, g + G_UP_B))
                    round_lb(1, 5, lb_count(5, blk))
                    silu(g + G_GATE_NEXT, 2 * blk + 2, 2 * blk + 2)
                    round_wt(S_BLOCK + 5, blk, 1, done(half, g + G_GATE_NEXT))
                    round_lb(0, 6, lb_count(6, blk))

                round_wd(S_DOWN_LAST, 0, 0, done(half, G_UP_LAST - 1), FULL - 1)
                round_act(0, 2 * BLOCKS)
                sc.wait_ge(groups_done, done(half, G_UP_LAST))
                round_lb(1, LB - 1, lb_count(LB - 1))
                round_wd(S_DOWN_TAIL, 0, 1, done(half, G_UP_LAST - 1), FULL)
                b_down_w = wt[0:3 * 2 * RANK, 0, :, :, :].rearrange("p c k m -> p c (k m)")
                for chunk in range(CHUNKS):
                    arrived(S_BDOWN + chunk, (half, 0))
                    copy(b_down_w[:, chunk, :], stage[0:3 * 2 * RANK, (S_BDOWN + chunk) % RING, :]
                         ).then_inc(rounded, 1)
                for chunk in range(CHUNKS):
                    sc.wait_ge(groups_done, done(half, G_TAIL, chunk))
                    sc.wait_ge(act_split, 4 * (BLOCKS + 1) * half + 4 * BLOCKS + chunk + 1)
                    nc.scalar.activation(tmp_s[0:TAIL, chunk, :], pair[0][0:TAIL, chunk, :], ACT.Silu)
                    copy(tmp_p[0:TAIL, chunk, :], pair[0][TAIL:2 * TAIL, chunk, :]).then_inc(pair_free[0], 1)
                for chunk in range(CHUNKS):
                    sc.wait_ge(tail_product, 2 * half + chunk + 1)
                    copy(act[0:TAIL, 1, HI, chunk * CH:(chunk + 1) * CH], tmp_p[0:TAIL, chunk, :]
                         ).then_inc(act_rounded, 1)
                round_wt(S_EXPERTS, 0, 1, done(half, G_TAIL))
                for chunk in range(CHUNKS):
                    rows, low = slice(64 * chunk, 64 * chunk + 32), slice(64 * chunk + 32, 64 * chunk + 64)
                    sc.wait_ge(pair_free[2], freed(2, half, FIRST4[2], chunk))
                    for b in range(2):
                        cols = slice(b * SEQ, (b + 1) * SEQ)
                        last = copy(tmp_s[rows, chunk, cols], ldown[low, cols], scale=scale_of[low, b:b + 1])
                    last.then_inc(lora_lo, 1)
                for chunk in range(CHUNKS):
                    rows = slice(64 * chunk, 64 * chunk + 32)
                    sc.wait_ge(lora_sum, 2 * half + chunk + 1)
                    own, other = (slice(0, 32), slice(64, 96)) if chunk == 0 else (slice(64, 96), slice(0, 32))
                    copy(ranks[own, chunk, 0, :], tmp_p[rows, chunk, :]).then_inc(lora_rounded, 1)
                    copy(ranks[other, chunk, 0, :], tmp_p[rows, chunk, :]).then_inc(lora_rounded, 1)
                for k in range(KT):
                    p, use = last_block(k + 1)
                    sc.wait_ge(pair_free[p], freed(p, half, use))
                    copy(xs[HI][:, k, :], resid[:, k, :]).then_inc(x_rounded, 1)
                sc.wait_ge(groups_done, done(half, G_DOWN_LAST + KT - 1))
                arrived(S_EXPERTS_B, (half, 0))
                copy(wd[:, 0, HI, :], stage[:, S_EXPERTS_B % RING, :]).then_inc(rounded, 1)
                round_wt(S_OUT, 0, 0, done(half, G_DOWN_LAST + KT - 1))
                for chunk in range(CHUNKS):
                    sc.wait_ge(groups_done, done(half, G_ROUTER, chunk))
                    copy(tmp_s[0:2 * EXPERTS, chunk, :], pair[3][0:2 * EXPERTS, chunk, :]).then_inc(pair_free[3], 1)
                round_wt(S_OUT + 1, 0, 1, done(half, G_EXPERTS))
                per_chunk = TT // CHUNKS
                for chunk in range(CHUNKS):
                    sc.wait_ge(groups_done, done(half, G_LOGITS_T, chunk))
                    copy(logits2[:, chunk * per_chunk:(chunk + 1) * per_chunk, :, :].rearrange("p t a e -> p (t a e)"),
                         pair[0][:, chunk, 0:per_chunk * 2 * EXPERTS]).then_inc(pair_free[0], 1)
                sc.wait_ge(route_step, ROUTE_STEPS * half + 4)
                nc.scalar.activation(odds[:, 1, :], odds[:, 0, :], ACT.Exp).then_inc(exp_ready, 1)
                for chunk in range(CHUNKS):
                    sc.wait_ge(groups_done, done(half, G_GATES_T, chunk))
                    copy(tmp_s[:, chunk, :], pair[0][:, chunk, :]).then_inc(pair_free[0], 1)
                round_wt(S_OUT + 2, 0, 0, done(half, G_GATES_T))
                for chunk in range(CHUNKS):
                    sc.wait_ge(pair_free[1], freed(1, half, U_EXPERTS, chunk))
                    copy(act[:, 0, HI, chunk * CH:(chunk + 1) * CH], tmp_p[:, chunk, :]).then_inc(hg_rounded, 1)
                for o in range(3, KT):
                    round_wt(S_OUT + o, 0, o % 2, done(half, G_GATES_T + o - 2))

        @block.vector
        def _(dve):
            def rest(dst, whole, high):
                return nc.vector.tensor_tensor(dst, whole, high.bitcast(F32), ALU.subtract)

            dve.sem_inc(split, RING)
            dve.sem_inc(lb_split, 2)
            for p in range(1, 4):
                dve.sem_inc(pair_free[p], 2)
            dve.wait_ge(const_in, 16 * 5)
            nc.vector.tensor_copy(lang[:, :], lang_i[:, :]).then_inc(lang_ready, 1)
            dve.wait_ge(lang_ready, 1)
            for n in range(NSEQ):
                last = nc.vector.tensor_scalar(lang_bias[:, n, :], expert[:, :], lang[:, n:n + 1], LANG_BIAS,
                                               ALU.is_equal, ALU.mult)
            last.then_inc(bias_ready, 1)
            dve.wait_ge(route_rounded, 1)
            rest(route_w[:, :, LO, :], route_raw[:, :, :], route_w[:, :, HI, :]).then_inc(route_ready, 1)

            with dve.Fori(0, HALVES) as half:
                stage0 = STAGES * half

                def rounded_by(n):
                    return (STAGES - 1) * half + n

                def rest_wt(k, n, slot):
                    dve.wait_ge(rounded, rounded_by(n))
                    rest(wt[:, slot, LO, :, :].rearrange("p k m -> p (k m)"), stage[:, k % RING, :],
                         wt[:, slot, HI, :, :].rearrange("p k m -> p (k m)")).then_inc(split, 1)

                def rest_lb(slot, e):
                    rows = slice(4 * RANK, 6 * RANK)
                    dve.wait_ge(lb_rounded, LB * half + e + 1)
                    rest(lbw[rows, slot, :, :], lb_raw[rows, slot, :, :], lbw[rows, slot, :, :]
                         ).then_inc(lb_split, 1)

                def rest_wd(k, n, t, tile):
                    dve.wait_ge(rounded, rounded_by(n))
                    rest(wd[:, t, LO, :], stage[:, k % RING, :], wd[:, t, HI, :])
                    by_part = ad[:, t, :].rearrange("p (c a b r) -> p c a b r", c=CHUNKS, a=2, b=2)
                    rest(by_part[:, :, LO, :, :],
                         ad_raw[:, :, bass.ds(tile, 1), :].rearrange("p (c b) o r -> p c b (o r)", c=CHUNKS),
                         by_part[:, :, HI, :, :]).then_inc(split, 1)

                def product(group, gate_use):
                    for chunk in range(CHUNKS):
                        dve.wait_ge(pair_free[0], freed(0, half, gate_use, chunk))
                        dve.wait_ge(groups_done, done(half, group, chunk))
                        nc.vector.tensor_tensor(tmp_p[:, chunk, :], tmp_s[:, chunk, :], pair[1][:, chunk, :],
                                                ALU.mult).then_inc(pair_free[1], 1)

                def rest_act(t, n):
                    for chunk in range(CHUNKS):
                        cols = slice(chunk * CH, (chunk + 1) * CH)
                        dve.wait_ge(act_rounded, 4 * (BLOCKS + 1) * half + 2 * n + chunk + 1)
                        rest(act[:, t, LO, cols], tmp_p[:, chunk, :], act[:, t, HI, cols]).then_inc(act_split, 1)

                def add_down(p, group, h):
                    for chunk in range(CHUNKS):
                        cols = slice(chunk * CH, (chunk + 1) * CH)
                        dve.wait_ge(groups_done, done(half, group, chunk))
                        nc.vector.tensor_tensor(resid[:, h, cols], resid[:, h, cols], pair[p][:, chunk, :],
                                                ALU.add).then_inc(pair_free[p], 1)

                def add_ldown(group):
                    for chunk in range(CHUNKS):
                        rows = slice(64 * chunk, 64 * chunk + 64)
                        dve.wait_ge(groups_done, done(half, group, chunk))
                        nc.vector.tensor_tensor(ldown[rows, :], ldown[rows, :], pair[2][rows, chunk, :],
                                                ALU.add).then_inc(pair_free[2], 1)

                def rest_x(n):
                    k = n % KT
                    dve.wait_ge(x_rounded, 2 * KT * half + n + 1)
                    rest(xs[LO][:, k, :], resid[:, k, :], xs[HI][:, k, :]).then_inc(x_split, 1)

                dve.wait_ge(groups_done, done_last_half(half, G_GATES_T + KT - 1))
                dve.wait_ge(stage_in[S_GU0 % RING], LOADED * (STAGES // RING) * half + LOADED)
                nc.vector.tensor_copy(wt[:, 1, HI, :, :].rearrange("p k m -> p (k m)"), stage[:, S_GU0 % RING, :]
                                      ).then_inc(gate0_rounded, 1)
                dve.wait_ge(rounded, (STAGES - 1) * half + 1)
                rank_w = wt[:, 0, :, :, :].rearrange("p c k (a g b r) -> p c k a g b r", a=2, g=2, b=2)
                raw = stage[:, 0, :].rearrange("p (c b k g r) -> p c b k g r", c=CHUNKS, b=2, k=KT, g=2)
                for chunk in range(CHUNKS):
                    for b in range(2):
                        last = rest(rank_w[:, chunk, :, LO, :, b, :], raw[:, chunk, b, :, :, :],
                                    rank_w[:, chunk, :, HI, :, b, :])
                last.then_inc(split, 1)
                for k in range(KT):
                    rest_x(k)
                nc.vector.memset(ldown[:, :], 0.0).then_inc(ldown_cleared, 1)
                dve.wait_ge(gate0_rounded, half + 1)
                rest(wt[:, 1, LO, :, :], stage[:, S_GU0 % RING, :].rearrange("p (k m) -> p k m", k=KT), wt[:, 1, HI, :, :]
                     ).then_inc(split, 1)
                for chunk in range(CHUNKS):
                    dve.wait_ge(lora_lo, 4 * half + chunk + 1)
                    dve.wait_ge(groups_done, done(half, G_RANK, chunk))
                    for b in range(2):
                        cols = slice(b * SEQ, (b + 1) * SEQ)
                        last = nc.vector.scalar_tensor_tensor(
                            out=tmp_p[0:64, chunk, cols], in0=pair[2][0:64, chunk, cols], scalar=scale_of[0:64, b:b + 1],
                            in1=tmp_s[0:64, chunk, cols], op0=ALU.mult, op1=ALU.add)
                    last.then_inc(pair_free[2], 1)
                for chunk in range(CHUNKS):
                    dve.wait_ge(pair_free[2], freed(2, half, 0, chunk))
                    nc.vector.tensor_copy(ranks[32:64, chunk, 1, :], tmp_p[32:64, chunk, :]).then_inc(lora_up_rounded, 1)
                    nc.vector.tensor_copy(ranks[64:96, chunk, 1, :], tmp_p[32:64, chunk, :])
                    dve.wait_ge(lora_rounded, 8 * half + 2 * chunk + 1)
                    rest(ranks[32:64, chunk, 0, :], tmp_p[0:32, chunk, :], ranks[0:32, chunk, 0, :])
                    dve.wait_ge(lora_rounded, 8 * half + 2 * chunk + 2)
                    dve.wait_ge(lora_up_rounded, 2 * half + chunk + 1)
                    rest(ranks[0:32, chunk, 1, :], tmp_p[32:64, chunk, :], ranks[32:64, chunk, 1, :]
                         ).then_inc(lora_split, 1)
                rest_wt(S_GU0 + 1, S_GU0 + 1, 0)
                rest_lb(0, 0)
                rest_lb(1, 1)
                rest_wt(S_GU0 + 2, S_GU0 + 2, 1)
                rest_lb(0, 2)

                with dve.Fori(0, BLOCKS) as blk:
                    st = STAGES_BLOCK * blk
                    g = PER_BLOCK * blk + G_BLOCK
                    rest_wd(S_BLOCK, S_BLOCK + st, 0, 2 * blk)
                    product(g + G_UP_A, 2 * blk)
                    rest_act(0, 2 * blk)
                    rest_wt(S_BLOCK + 1, S_BLOCK + 1 + st, 0)
                    rest_lb(1, 4 * blk + 3)
                    rest_wt(S_BLOCK + 2, S_BLOCK + 2 + st, 1)
                    rest_lb(0, 4 * blk + 4)
                    rest_wd(S_BLOCK + 3, S_BLOCK + 3 + st, 1, 2 * blk + 1)
                    product(g + G_UP_B, 2 * blk + 1)
                    rest_act(1, 2 * blk + 1)
                    rest_wt(S_BLOCK + 4, S_BLOCK + 4 + st, 0)
                    rest_lb(1, 4 * blk + 5)
                    dve.wait_ge(ldown_cleared, half + 1)
                    dve.wait_ge(pair_free[2], free_for(2, half, 5 * blk + 1))
                    dve.wait_ge(pair_free[3], free_for(3, half, 4 * blk))
                    add_ldown(g + G_LDOWN)
                    for h in range(KT):
                        add_down(3 - h % 2, g + G_DOWN + h, h)
                        if h == 1:
                            rest_wt(S_BLOCK + 5, S_BLOCK + 5 + st, 1)
                            rest_lb(0, 4 * blk + 6)

                rest_wd(S_DOWN_LAST, S_DOWN_LAST, 0, FULL - 1)
                product(G_UP_LAST, 2 * BLOCKS)
                rest_act(0, 2 * BLOCKS)
                rest_lb(1, LB - 1)
                rest_wd(S_DOWN_TAIL, S_DOWN_TAIL, 1, FULL)
                b_down_w = wt[4 * RANK:6 * RANK, 0, :, :, :].rearrange("p c k m -> p c (k m)")
                for chunk in range(CHUNKS):
                    n = S_BDOWN + chunk
                    dve.wait_ge(rounded, rounded_by(n))
                    rest(b_down_w[:, chunk, :], stage[4 * RANK:6 * RANK, n % RING, :], b_down_w[:, chunk, :]
                         ).then_inc(split, 1)
                for chunk in range(CHUNKS):
                    dve.wait_ge(pair_free[0], freed(0, half, U_TAIL, chunk))
                    nc.vector.tensor_tensor(tmp_p[0:TAIL, chunk, :], tmp_s[0:TAIL, chunk, :],
                                            tmp_p[0:TAIL, chunk, :], ALU.mult).then_inc(tail_product, 1)
                for chunk in range(CHUNKS):
                    cols = slice(chunk * CH, (chunk + 1) * CH)
                    dve.wait_ge(act_rounded, 4 * (BLOCKS + 1) * half + 4 * BLOCKS + 2 + chunk + 1)
                    rest(act[TAIL:2 * TAIL, 1, HI, cols], tmp_p[0:TAIL, chunk, :], act[0:TAIL, 1, HI, cols]
                         ).then_inc(act_split, 1)
                dve.wait_ge(pair_free[2], free_for(2, half, FIRST4[2]))
                dve.wait_ge(pair_free[3], free_for(3, half, FIRST4[3]))
                add_ldown(G_LDOWN_LAST)
                for chunk in range(CHUNKS):
                    rows = slice(64 * chunk, 64 * chunk + 32)
                    dve.wait_ge(lora_lo, 4 * half + 2 + chunk + 1)
                    for b in range(2):
                        cols = slice(b * SEQ, (b + 1) * SEQ)
                        last = nc.vector.scalar_tensor_tensor(
                            out=tmp_p[rows, chunk, cols], in0=ldown[rows, cols], scalar=scale_of[rows, b:b + 1],
                            in1=tmp_s[rows, chunk, cols], op0=ALU.mult, op1=ALU.add)
                    last.then_inc(lora_sum, 1)
                for chunk in range(CHUNKS):
                    rows = slice(64 * chunk, 64 * chunk + 32)
                    dve.wait_ge(lora_rounded, 8 * half + 4 + 2 * chunk + 2)
                    rest(ranks[32:64, chunk, 0, :], tmp_p[rows, chunk, :], ranks[rows, chunk, 0, :]
                         ).then_inc(lora_split, 1)
                rest_wt(S_EXPERTS, S_EXPERTS, 1)
                for h in range(KT):
                    add_down(last_block(h + 1)[0], G_DOWN_LAST + h, h)
                    if h:
                        rest_x(KT + h - 1)
                rest_x(2 * KT - 1)
                dve.wait_ge(rounded, rounded_by(S_EXPERTS_B))
                rest(wd[:, 0, LO, :], stage[:, S_EXPERTS_B % RING, :], wd[:, 0, HI, :]).then_inc(split, 1)
                rest_wt(S_OUT, S_OUT, 0)
                rest_wt(S_OUT + 1, S_OUT + 1, 1)

                def link(instruction, step):
                    instruction.then_inc(route_step, 1)
                    if step < ROUTE_STEPS:
                        dve.wait_ge(route_step, ROUTE_STEPS * half + step)

                def over(ap, n):
                    return ap.unsqueeze(ap.ndim).to_broadcast(list(ap.shape) + [n])

                dve.wait_ge(bias_ready, 1)
                dve.wait_ge(pair_free[0], freed(0, half, U_LOGITS_T))
                link(nc.vector.tensor_tensor(logits[:, :, :], logits2[:, :, HI, :], logits2[:, :, LO, :], ALU.add), 1)
                for t in range(TT // SEQ_HALF):
                    by_seq = logits[:, :, :].rearrange("p (s t) e -> p s t e", t=TT // SEQ_HALF)[:, :, t, :]
                    last = nc.vector.tensor_tensor(by_seq, by_seq, lang_bias[:, bass.ds(SEQ_HALF * half, SEQ_HALF), :],
                                                   ALU.add)
                link(last, 2)
                nc.vector.tensor_reduce(highest[:, :], logits[:, :, :], mybir.AxisListType.X, ALU.max)
                for t in range(TT):
                    last = nc.vector.max(best[:, t, :], logits[:, t, :])
                link(last, 3)
                nc.vector.tensor_tensor(odds[:, 0, :], best[:, :, 1], highest[:, :], ALU.subtract
                                        ).then_inc(route_step, 1)
                for t in range(TT):
                    last = nc.vector.max_index(best_at[:, t, :], best[:, t, :], logits[:, t, :])
                link(last, 5)
                nc.vector.tensor_copy(best_no[:, :, :], best_at[:, :, 0:2])
                dve.wait_ge(exp_ready, half + 1)
                link(nc.vector.tensor_scalar(weight[:, 0, :], odds[:, 1, :], 1.0, None, ALU.add), 6)
                link(nc.vector.reciprocal(weight[:, 1, :], weight[:, 0, :]), 7)
                link(nc.vector.tensor_scalar(weight[:, 2, :], weight[:, 1, :], SCALING, None, ALU.mult), 8)
                nc.vector.tensor_tensor(weight[:, 3, :], weight[:, 2, :], odds[:, 1, :], ALU.mult)
                numbers = expert[:, :].unsqueeze(1).to_broadcast([P, TT, EXPERTS])
                for i in range(2):
                    last = nc.vector.tensor_tensor(picked[:, i, :, :], numbers, over(best_no[:, :, i], EXPERTS),
                                                   ALU.is_equal)
                link(last, 9)
                for i in range(2):
                    last = nc.vector.tensor_tensor(picked[:, i, :, :], picked[:, i, :, :],
                                                   over(weight[:, 2 + i, :], EXPERTS), ALU.mult)
                link(last, 10)
                by_token = picked[:, :, :, :].rearrange("p i t e -> p i (t e)")
                link(nc.vector.tensor_tensor(
                    tmp_p[:, :, :].rearrange("p c n -> p (c n)").rearrange("p (n r) -> p n r", r=RANK),
                    over(by_token[:, 0, :], RANK), over(by_token[:, 1, :], RANK), ALU.add), 11)

                for chunk in range(CHUNKS):
                    dve.wait_ge(pair_free[0], freed(0, half, U_GATES_T, chunk))
                    nc.vector.tensor_tensor(tmp_p[:, chunk, :], tmp_s[:, chunk, :], pair[1][:, chunk, :],
                                            ALU.mult).then_inc(pair_free[1], 1)
                for chunk in range(CHUNKS):
                    cols = slice(chunk * CH, (chunk + 1) * CH)
                    dve.wait_ge(hg_rounded, 2 * half + chunk + 1)
                    rest(act[:, 0, LO, cols], tmp_p[:, chunk, :], act[:, 0, HI, cols]).then_inc(hg_split, 1)
                rest_wt(S_OUT + 2, S_OUT + 2, 0)
                for o in range(KT):
                    if o + 3 < KT:
                        rest_wt(S_OUT + o + 3, S_OUT + o + 3, (o + 3) % 2)
                    add_down(RING3[o % 3], G_OUT + o, o)


_OUT = (HALVES, KT, P, NT)


def kernel(**inputs):
    import numpy as np
    import concourse.bacc as bacc
    from concourse.bass_utils import run_bass_kernel_spmd

    v = {name: np.asarray(a) for name, a in inputs.items()}

    def width_tiles(w):
        return np.ascontiguousarray(w.reshape(-1, P, KT, P).transpose(0, 3, 2, 1)).reshape(-1, P, D)

    gate, up = v["L0_cond_W_gate"], v["L0_cond_W_up"]
    full = FULL * P
    pairs = np.stack([gate[:full].reshape(FULL, P, D), up[:full].reshape(FULL, P, D)], 1).reshape(-1, D)
    w_gu = width_tiles(np.concatenate([pairs, gate[full:], up[full:]]))
    down_t = v["L0_cond_W_down"].T
    w_down = np.concatenate([down_t, down_t[full:]]).reshape(FT, P, D)
    a_g, a_u = v["L0_cond_A_gate"][0], v["L0_cond_A_up"][0]
    a_gu = np.stack([a_g, a_u], 1).reshape(ADAPTERS, 2, RANK, KT, P).transpose(0, 4, 3, 1, 2).reshape(ADAPTERS, P, -1)
    b_g, b_u = (v[n][0].transpose(0, 2, 1) for n in ("L0_cond_B_gate", "L0_cond_B_up"))
    b_gu = np.zeros((ADAPTERS, RANK, LB, P), b_g.dtype)
    b_gu[:, :, 0:2 * FULL:2] = b_g[:, :, :full].reshape(ADAPTERS, RANK, FULL, P)
    b_gu[:, :, 1:2 * FULL:2] = b_u[:, :, :full].reshape(ADAPTERS, RANK, FULL, P)
    b_gu[:, :, LB - 2, :TAIL] = b_g[:, :, full:]
    b_gu[:, :, LB - 1, TAIL:] = b_u[:, :, full:]
    a_d = v["L0_cond_A_down"][0]
    a_down = np.concatenate([a_d, a_d[:, :, full:]], 2).reshape(ADAPTERS, RANK, FT, P)
    a_down = a_down.transpose(0, 3, 2, 1).reshape(ADAPTERS, P, FT * RANK)
    tokens = v["x"].reshape(HALVES, NT, KT, P)
    rows = np.arange(P)
    arrays = {
        "x_t": tokens.transpose(0, 2, 3, 1),
        "w_gu": w_gu,
        "w_down": w_down,
        "a_gu": a_gu,
        "b_gu": b_gu,
        "a_down": a_down,
        "b_down": v["L0_cond_B_down"][0].transpose(0, 2, 1),
        "w_out": width_tiles(v["L1_cond_W"]),
        "a_exp": width_tiles(v["L1_cond_A"].reshape(EXPERTS * RANK, D))[0],
        "b_exp": v["L1_cond_B"].transpose(0, 2, 1).reshape(EXPERTS * RANK, D),
        "w_route": v["L1_cond_Wr"].reshape(EXPERTS, KT, P).transpose(2, 1, 0),
        "adapter_of": v["itok_B_2_6"].reshape(1, NSEQ),
        "language_of": v["itok_B_0_7"].reshape(1, NSEQ),
        "identity": np.eye(P, dtype=np.float32),
        "seq_scale": np.stack([np.where(rows // RANK % 2 == b, LORA_SCALE, 0.0) for b in range(2)], 1).astype(np.float32),
        "expert_no": np.tile(np.arange(EXPERTS, dtype=np.float32), (P, 1)),
    }
    arrays = {name: np.ascontiguousarray(a) for name, a in arrays.items()}
    nc = bacc.Bacc("TRN2", target_bir_lowering=False, num_devices=1)
    args = [nc.dram_tensor(n, a.shape, mybir.dt.from_np(a.dtype), kind="ExternalInput").ap() for n, a in arrays.items()]
    args.append(nc.dram_tensor("out", _OUT, F32, kind="ExternalOutput").ap())
    cond_resid_kernel(nc, *args)
    got = run_bass_kernel_spmd(nc, [arrays], core_ids=[0]).results[0]["out"]
    return np.ascontiguousarray(got.transpose(0, 3, 1, 2)).reshape(NSEQ, SEQ, D)
```

```python
from contextlib import ExitStack

import concourse.bass as bass
from concourse import mybir

P = 128
D = 1024
F = 2752
KT = D // P
FULL = F // P
TAIL = F - FULL * P
FT = FULL + 1
SEQ = 256
NSEQ = 8
HALVES = 2
SEQ_HALF = NSEQ // HALVES
CHUNKS = 2
CH = 2 * SEQ
NT = CHUNKS * CH
RANK = 16
ADAPTERS = 16
EXPERTS = 8
LANG_BIAS = 5.0
SCALING = 2.0
LORA_SCALE = 0.5
GU = 2 * FULL + 1
LB = GU + 1
BLOCKS = (FULL - 1) // 2

G_RANK, G_GATE0, G_BLOCK, PER_BLOCK = 0, 1, 2, 13
G_UP_A, G_GATE_B, G_UP_B, G_GATE_NEXT, G_LDOWN, G_DOWN = 0, 1, 2, 3, 4, 5
G_UP_LAST = G_BLOCK + PER_BLOCK * BLOCKS
G_TAIL = G_UP_LAST + 1
G_LDOWN_LAST = G_TAIL + 1
G_DOWN_LAST = G_LDOWN_LAST + 1
G_ROUTER = G_DOWN_LAST + KT
G_EXPERTS = G_ROUTER + 1
G_LOGITS_T = G_EXPERTS + 1
G_GATES_T = G_LOGITS_T + 1
G_OUT = G_GATES_T + 1
GROUPS = G_OUT + KT

S_GATE0, S_RANK, S_UP0, S_GATE1, S_BLOCK, STAGES_BLOCK = 0, 1, 2, 3, 4, 6
S_DOWN_LAST = S_BLOCK + STAGES_BLOCK * BLOCKS
S_DOWN_TAIL = S_DOWN_LAST + 1
S_BDOWN = S_DOWN_TAIL + 1
S_EXPERTS = S_BDOWN + 2
S_EXPERTS_B = S_EXPERTS + 1
S_OUT = S_EXPERTS_B + 1
STAGES = S_OUT + KT
RING = 3
LOADED = 96
assert STAGES % RING == 0 and LB % 2 == 0

USES = (2 * BLOCKS + 6, 2 * BLOCKS + 6, 5 * BLOCKS + 7, 4 * BLOCKS + 6)
RING4 = (2, 3, 1, 0)
FIRST4 = {2: 5 * BLOCKS + 1, 3: 4 * BLOCKS, 1: 2 * BLOCKS + 1, 0: 2 * BLOCKS + 2}
RING3 = (2, 3, 1)
FIRST3 = {2: 5 * BLOCKS + 4, 3: 4 * BLOCKS + 3, 1: 2 * BLOCKS + 4}
U_TAIL = 2 * BLOCKS + 1
U_ROUTER = 4 * BLOCKS + 2
U_EXPERTS = 2 * BLOCKS + 3
U_LOGITS_T = 2 * BLOCKS + 4
U_GATES_T = 2 * BLOCKS + 5


def last_block(j):
    p = RING4[j % 4]
    return p, FIRST4[p] + j // 4


def out_tile(o):
    p = RING3[o % 3]
    return p, FIRST3[p] + o // 3


ROUTE_STEPS = 11

ALU = mybir.AluOpType
ACT = mybir.ActivationFunctionType
F32 = mybir.dt.float32
F32R = mybir.dt.float32r
I32 = mybir.dt.int32
U32 = mybir.dt.uint32

HI, LO = 0, 1
SPLITS_X = 2 * KT - 1
RANKS_AT = 6
EARLY = 2
LOW_LAG = 3
LORA_AT = 5
PASSES = ((HI, HI), (HI, LO), (LO, HI))
RANK_PASSES = (HI, LO)


def cond_resid_kernel(nc, x_t, w_gu, w_down, a_gu, b_gu, a_down, b_down, w_out, a_exp, b_exp, w_route,
                      adapter_of, language_of, identity, seq_scale, expert_no, out):
    with ExitStack() as ctx:
        def sb(name, shape, dt=F32):
            return ctx.enter_context(nc.sbuf_tensor(name, shape, dt))

        def sem(name):
            return ctx.enter_context(nc.semaphore(name))

        lb_dram = nc.dram_tensor("lb_dram", (HALVES, LB, 2 * RANK, CHUNKS, P), F32).ap()

        xs = [sb("x_hi", [P, KT, NT], F32R), sb("x_lo", [P, KT, NT], F32R)]
        resid = sb("resid", [P, KT, NT])
        act = sb("act", [P, 2, 2, NT], F32R)
        wd = sb("wd", [P, 2, 2, D], F32R)
        ad = sb("ad", [P, 2, P], F32R)
        wt = sb("wt", [P, 2, 2, KT, P], F32R)
        stage = sb("stage", [P, RING, D])
        lb_raw = sb("lb_raw", [3 * 2 * RANK, 2, CHUNKS, P])
        lbw = sb("lbw", [3 * 2 * RANK, 2, CHUNKS, P], F32R)
        ranks = sb("ranks", [3 * 2 * RANK, CHUNKS, 2, CH], F32R)
        ldown = sb("ldown", [P, CH])
        ad_raw = sb("ad_raw", [P, SEQ_HALF, FT, RANK])
        tmp_s = sb("tmp_s", [P, CHUNKS, CH])
        tmp_p = sb("tmp_p", [P, CHUNKS, CH])
        route_raw = sb("route_raw", [P, KT, EXPERTS])
        route_w = sb("route_w", [P, KT, 2, EXPERTS], F32R)
        ident = sb("ident", [P, P])
        scale_of = sb("scale_of", [P, 2])
        expert = sb("expert", [P, EXPERTS])
        adapters = sb("adapters", [1, NSEQ], I32)
        lang_i = sb("lang_i", [P, NSEQ], I32)
        lang = sb("lang", [P, NSEQ])
        lang_bias = sb("lang_bias", [P, NSEQ, EXPERTS])
        TT = NT // P
        logits2 = sb("logits2", [P, TT, 2, EXPERTS])
        logits = sb("logits", [P, TT, EXPERTS])
        best = sb("best", [P, TT, 8])
        best_at = sb("best_at", [P, TT, 8], U32)
        best_no = sb("best_no", [P, TT, 2])
        highest = sb("highest", [P, TT])
        odds = sb("odds", [P, 2, TT])
        weight = sb("weight", [P, 4, TT])
        picked = sb("picked", [P, 2, TT, EXPERTS])

        pair = [ctx.enter_context(nc.psum_tensor(f"pair{i}", [P, CHUNKS, CH], F32)) for i in range(4)]

        const_in = sem("const_in")
        adapters_in = sem("adapters_in")
        lb_gathered = sem("lb_gathered")
        stage_in = [sem(f"stage_in{i}") for i in range(RING)]
        lb_in = [sem(f"lb_in{i}") for i in range(2)]
        ad_in = sem("ad_in")
        x_in = [sem(f"x_in{k}") for k in range(KT)]
        out_stored = [sem(f"out_stored{k}") for k in range(KT)]
        rounded = sem("rounded")
        split = sem("split")
        lb_rounded = sem("lb_rounded")
        lb_split = sem("lb_split")
        xs_free = sem("xs_free")
        x_rounded = sem("x_rounded")
        x_split = sem("x_split")
        x0_split = sem("x0_split")
        groups_done = sem("groups_done")
        pair_free = [sem(f"pair_free{i}") for i in range(4)]
        act_rounded = sem("act_rounded")
        act_split = sem("act_split")
        tail_product = sem("tail_product")
        ldown_cleared = sem("ldown_cleared")
        lora_lo = sem("lora_lo")
        lora_sum = sem("lora_sum")
        lora_rounded = sem("lora_rounded")
        lora_up_rounded = sem("lora_up_rounded")
        lora_split = sem("lora_split")
        route_rounded = sem("route_rounded")
        route_ready = sem("route_ready")
        lang_ready = sem("lang_ready")
        bias_ready = sem("bias_ready")
        route_step = sem("route_step")
        exp_ready = sem("exp_ready")
        hg_rounded = sem("hg_rounded")
        hg_split = sem("hg_split")

        def done(half, group, chunk=1):
            return 2 * GROUPS * half + (2 * GROUPS + 2 * group + chunk + 1)

        def done_last_half(half, group):
            return 2 * GROUPS * half + (2 * group + 2)

        def freed(p, half, use, chunk=1):
            return 2 * USES[p] * half + 2 * use + (chunk + 3)

        def free_for(p, half, use, chunk=1):
            return 2 * USES[p] * half + 2 * use + (chunk + 1)

        block = ctx.enter_context(nc.Block())

        @block.gpsimd
        def _(pool):
            def stored(halves, k):
                return halves * (32 if k == KT - 1 else 16)

            def load_x(half, k):
                if half:
                    pool.wait_ge(out_stored[k], stored(half, k))
                pool.dma_start(resid[:, k, :], x_t[half, k]).then_inc(x_in[k], 16)

            def gather_lb(half):
                pool.wait_ge(adapters_in, 16)
                for s in range(SEQ_HALF):
                    chunk, b = divmod(s, 2)
                    n = half * SEQ_HALF + s
                    a = pool.value_load(adapters[0:1, n:n + 1], min_val=0, max_val=ADAPTERS - 1)
                    src = b_gu[bass.ds(a, 1)].rearrange("o r t f -> (o r) t f")
                    dst = lb_dram[half, :, b * RANK:(b + 1) * RANK, chunk, :].rearrange("t r f -> r t f")
                    pool.dma_start(dst, src).then_inc(lb_gathered, 16)
                pool.wait_ge(lb_gathered, 16 * SEQ_HALF * (half + 1))

            def store_out(half, o):
                p, use = out_tile(o)
                for chunk in range(CHUNKS):
                    if o < KT - 1 and chunk == 0:
                        continue
                    cols = slice(chunk * CH if o == KT - 1 else 0, (chunk + 1) * CH)
                    pool.wait_ge(pair_free[p], freed(p, half, use, chunk))
                    pool.dma_start(out[half, o, :, cols], resid[:, o, cols]).then_inc(out_stored[o], 16)

            def split_ranks(half):
                rank_w = wt[:, 0, :, :, :].rearrange("p c k (a g b r) -> p c k a g b r", a=2, g=2, b=2)
                raw = stage[:, S_RANK, :].rearrange("p (c b k g r) -> p c b k g r", c=CHUNKS, b=2, k=KT, g=2)
                pool.wait_ge(rounded, STAGES * half + S_RANK + 1)
                pool.wait_ge(split, STAGES * half + S_RANK + RING)
                for chunk in range(CHUNKS):
                    for b in range(2):
                        last = nc.gpsimd.tensor_tensor(rank_w[:, chunk, :, LO, :, b, :], raw[:, chunk, b, :, :, :],
                                                       rank_w[:, chunk, :, HI, :, b, :].bitcast(F32), ALU.subtract)
                last.then_inc(split, 1)

            def split_experts(half):
                pool.wait_ge(split, STAGES * half + S_EXPERTS + RING)
                pool.wait_ge(rounded, STAGES * half + S_EXPERTS + 1)
                nc.gpsimd.tensor_tensor(wt[:, 0, LO, :, :].rearrange("p k m -> p (k m)"), stage[:, S_EXPERTS % RING, :],
                                        wt[:, 0, HI, :, :].rearrange("p k m -> p (k m)").bitcast(F32), ALU.subtract
                                        ).then_inc(split, 1)

            def split_x0(half):
                pool.wait_ge(x_rounded, 2 * KT * half + KT + 1)
                nc.gpsimd.tensor_tensor(xs[LO][:, 0, :], resid[:, 0, :], xs[HI][:, 0, :].bitcast(F32), ALU.subtract
                                        ).then_inc(x0_split, 1)

            def split_b_down(half):
                low_rows = slice(4 * RANK, 6 * RANK)
                b_down_w = wt[low_rows, 1, :, :, :].rearrange("p c k m -> p c (k m)")
                for chunk in range(CHUNKS):
                    n = S_BDOWN + chunk
                    pool.wait_ge(rounded, STAGES * half + n + 1)
                    if chunk == 0:
                        pool.wait_ge(split, STAGES * half + n + RING)
                    nc.gpsimd.tensor_tensor(b_down_w[:, chunk, :], stage[low_rows, n % RING, :],
                                            b_down_w[:, chunk, :].bitcast(F32), ALU.subtract).then_inc(split, 1)

            for k in range(KT):
                load_x(0, k)
            pool.dma_start(scale_of[:, :], seq_scale).then_inc(const_in, 16)
            pool.dma_start(route_raw[:, :, :], w_route).then_inc(const_in, 16)
            pool.dma_start(lang_i[:, :], language_of.to_broadcast([P, NSEQ])).then_inc(const_in, 16)
            pool.dma_start(expert[:, :], expert_no).then_inc(const_in, 16)
            pool.dma_start(ident[:, :], identity).then_inc(const_in, 16)
            split_ranks(0)
            gather_lb(0)
            gather_lb(1)
            pool.wait_ge(const_in, 16 * 5)
            nc.gpsimd.tensor_copy(lang[:, :], lang_i[:, :]).then_inc(lang_ready, 1)
            pool.wait_ge(lang_ready, 1)
            for n in range(NSEQ):
                last = nc.gpsimd.tensor_scalar(lang_bias[:, n, :], expert[:, :], lang[:, n:n + 1], LANG_BIAS,
                                               ALU.is_equal, ALU.mult)
            last.then_inc(bias_ready, 1)
            nc.gpsimd.tensor_copy(route_w[:, :, HI, :], route_raw[:, :, :]).then_inc(route_rounded, 1)
            pool.wait_ge(route_rounded, 1)
            nc.gpsimd.tensor_tensor(route_w[:, :, LO, :], route_raw[:, :, :], route_w[:, :, HI, :].bitcast(F32), ALU.subtract
                                    ).then_inc(route_ready, 1)
            pool.wait_ge(route_ready, 1)
            split_b_down(0)
            split_experts(0)
            split_x0(0)
            for o in range(KT - 1):
                store_out(0, o)
                if o >= 2:
                    load_x(1, o - 2)
            load_x(1, KT - 3)
            load_x(1, KT - 2)
            store_out(0, KT - 1)
            split_ranks(1)
            load_x(1, KT - 1)
            pool.wait_ge(split, STAGES + S_UP0 + RING)
            split_b_down(1)
            split_experts(1)
            split_x0(1)
            for o in range(KT):
                store_out(1, o)
            for k in range(KT):
                pool.wait_ge(out_stored[k], stored(HALVES, k))

        @block.sync
        def _(sp):
            with sp.Fori(0, HALVES) as half:
                stage0 = STAGES * half

                def slot_free(n):
                    sp.wait_ge(split, n + 1)

                def adapter(s):
                    return sp.value_load(adapters[0:1, bass.ds(SEQ_HALF * half + s, 1)],
                                         min_val=0, max_val=ADAPTERS - 1)

                def load(k, base, src):
                    slot_free(base + k)
                    sp.dma_start(stage[:, k % RING, :], src).then_inc(stage_in[k % RING], LOADED)

                def load_lb(e):
                    sp.wait_ge(lb_split, LB * half + e + 1)
                    return e

                def lb_dmas(slot, e):
                    for part in range(3):
                        rows = slice(part * 2 * RANK, (part + 1) * 2 * RANK)
                        sp.dma_start(lb_raw[rows, slot, :, :],
                                     lb_dram[bass.ds(half, 1), bass.ds(e, 1)].rearrange("a b r c f -> (a b r) c f")
                                     ).then_inc(lb_in[slot], 16)

                def one(t, n):
                    return t[bass.ds(n, 1)].rearrange("o p n -> (o p) n")

                load(S_GATE0, stage0, w_gu[0])
                sp.wait_ge(adapters_in, 16)
                of = [adapter(s) for s in range(SEQ_HALF)]
                slot_free(stage0 + S_RANK)
                for s in range(SEQ_HALF):
                    sp.dma_start(stage[:, S_RANK, s * 256:(s + 1) * 256], one(a_gu, of[s])
                                 ).then_inc(stage_in[S_RANK], 32 if s % 2 else 16)
                sp.wait_ge(x_in[KT - 3], 16)
                load(S_UP0, stage0, w_gu[1])
                for s in range(SEQ_HALF):
                    sp.dma_start(ad_raw[:, s, :, :].rearrange("p t r -> p (t r)"), one(a_down, of[s])
                                 ).then_inc(ad_in, 16)
                sp.wait_ge(lb_gathered, 16 * SEQ_HALF * half + 16 * SEQ_HALF)
                for e in range(3):
                    load_lb(e)
                    lb_dmas(e % 2, e)
                    if e == 1:
                        load(S_GATE1, stage0, w_gu[2])

                with sp.Fori(0, BLOCKS) as blk:
                    base = stage0 + STAGES_BLOCK * blk
                    tile = 4 * blk
                    load(S_BLOCK + 0, base, one(w_down, 2 * blk))
                    load(S_BLOCK + 1, base, one(w_gu, tile + 3))
                    load_lb(tile + 3)
                    lb_dmas(1, tile + 3)
                    load(S_BLOCK + 2, base, one(w_gu, tile + 4))
                    load_lb(tile + 4)
                    lb_dmas(0, tile + 4)
                    load(S_BLOCK + 3, base, one(w_down, 2 * blk + 1))
                    load(S_BLOCK + 4, base, one(w_gu, tile + 5))
                    load_lb(tile + 5)
                    lb_dmas(1, tile + 5)
                    load(S_BLOCK + 5, base, one(w_gu, tile + 6))
                    load_lb(tile + 6)
                    lb_dmas(0, tile + 6)

                load(S_DOWN_LAST, stage0, w_down[FULL - 1])
                load_lb(LB - 1)
                lb_dmas(1, LB - 1)
                load(S_DOWN_TAIL, stage0, w_down[FULL])
                for chunk in range(CHUNKS):
                    n = S_BDOWN + chunk
                    slot_free(stage0 + n)
                    for b in range(2):
                        for part in range(3):
                            row = part * 2 * RANK + b * RANK
                            sp.dma_start(stage[row:row + RANK, n % RING, :], one(b_down, of[2 * chunk + b])
                                         ).then_inc(stage_in[n % RING], 16)
                load(S_EXPERTS, stage0, a_exp)
                load(S_EXPERTS_B, stage0, b_exp)
                for o in range(KT):
                    load(S_OUT + o, stage0, w_out[o])

        @block.tensor
        def _(pe):
            pe.sem_inc(groups_done, 2 * GROUPS)
            pe.sem_inc(xs_free, KT - 1)
            with pe.Fori(0, HALVES) as half:

                def stages_ready(n):
                    pe.wait_ge(split, STAGES * half + n + (RING + 1))

                def banks_free(p, use):
                    pe.wait_ge(pair_free[p], free_for(p, half, use))

                def columns(chunk):
                    return slice(chunk * CH, (chunk + 1) * CH)

                def width_pass(p, slot, k, w, a, start=False, stop=False):
                    for chunk in range(CHUNKS):
                        mm = nc.tensor.matmul(pair[p][:, chunk, :], wt[:, slot, w, k, :], xs[a][:, k, columns(chunk)],
                                              start=start, stop=stop)
                        if stop:
                            mm.then_inc(groups_done, 1)
                    return mm

                def width_product(p, use, slot, stop, also_wait=None):
                    banks_free(p, use)
                    for k in range(KT):
                        if also_wait and k == KT // 2:
                            also_wait()
                        for w, a in PASSES:
                            width_pass(p, slot, k, w, a, start=(k == 0 and (w, a) == (HI, HI)),
                                       stop=(stop and k == KT - 1 and w == LO))

                def lora_tile(p, e, slot, side, last=True):
                    pe.wait_ge(lb_split, LB * half + e + 3)
                    for chunk in range(CHUNKS):
                        mm = nc.tensor.matmul(pair[p][:, chunk, :], lbw[:, slot, chunk, :],
                                              ranks[:, chunk, side, :], start=False, stop=last)
                        if last:
                            mm.then_inc(groups_done, 1)

                def gate_or_up(p, use, n, e, side):
                    stages_ready(n)
                    width_product(p, use, 1 - side, stop=False)
                    lora_tile(p, e, side, side)

                def down_product(p, h, t, tail, stop):
                    if not tail:
                        parts = [(wd[:, t, w, h * P:(h + 1) * P], act[:, t, a]) for w, a in PASSES]
                    else:
                        parts = [(wd[:, t, HI, h * P:(h + 1) * P], act[:, t, HI]),
                                 (wd[0:TAIL, t, LO, h * P:(h + 1) * P], act[0:TAIL, t, HI])]
                    for i, (weights, values) in enumerate(parts):
                        for chunk in range(CHUNKS):
                            last = stop and i == len(parts) - 1
                            mm = nc.tensor.matmul(pair[p][:, chunk, :], weights, values[:, columns(chunk)],
                                                  start=(t == 0 and i == 0), stop=last)
                            if last:
                                mm.then_inc(groups_done, 1)

                def lora_down(p, t, tail):
                    for a in RANK_PASSES[:1 if tail else 2]:
                        for chunk in range(CHUNKS):
                            last = t == 1 and (tail or a == LO)
                            mm = nc.tensor.matmul(pair[p][:, chunk, :], ad[:, t, :], act[:, t, a, columns(chunk)],
                                                  start=(t == 0 and a == HI), stop=last)
                            if last:
                                mm.then_inc(groups_done, 1)

                rank_w = wt[:, 0, :, :, :].rearrange("p c k m -> p (c k) m")

                def rank_pass(k, a):
                    for chunk in range(CHUNKS):
                        mm = nc.tensor.matmul(pair[2][:, chunk, :], rank_w[:, chunk * KT + k, :],
                                              xs[a][:, k, columns(chunk)],
                                              start=(k == 0 and a == HI), stop=(k == KT - 1 and a == LO))
                        if k == KT - 1 and a == LO:
                            mm.then_inc(groups_done, 1)

                def gate0_pass(k, w):
                    if w == HI:
                        pe.wait_ge(x_rounded, 2 * KT * half + k + 1)
                    elif k == 0:
                        stages_ready(S_GATE0)
                    width_pass(0, 1, k, w, HI, start=(k == 0 and w == HI))

                pe.wait_ge(rounded, STAGES * half + S_GATE0 + 1)
                banks_free(0, 0)
                for k in range(KT - 1):
                    gate0_pass(k, HI)
                    if k >= LOW_LAG:
                        gate0_pass(k - LOW_LAG, LO)
                    if k > LOW_LAG and k - LOW_LAG - 1 < EARLY:
                        pe.wait_ge(x_split, SPLITS_X * half + k - LOW_LAG)
                        width_pass(0, 1, k - LOW_LAG - 1, HI, LO)
                for k in range(KT - 1 - LOW_LAG, KT - 1):
                    gate0_pass(k, LO)
                stages_ready(S_RANK)
                banks_free(2, 0)
                for k in range(KT - 1):
                    rank_pass(k, HI)
                for k in range(KT - 1):
                    pe.wait_ge(x_split, SPLITS_X * half + k + 1)
                    rank_pass(k, LO)
                gate0_pass(KT - 1, HI)
                gate0_pass(KT - 1, LO)
                rank_pass(KT - 1, HI)
                pe.wait_ge(x_split, SPLITS_X * half + KT)
                rank_pass(KT - 1, LO)
                for k in range(EARLY, KT):
                    width_pass(0, 1, k, HI, LO)
                stages_ready(S_UP0)
                banks_free(1, 0)
                for k in range(KT):
                    if k == LORA_AT:
                        pe.wait_ge(lora_split, 4 * half + 2)
                        lora_tile(0, 0, 0, 0)
                    for w, a in PASSES:
                        width_pass(1, 0, k, w, a, start=(k == 0 and (w, a) == (HI, HI)))
                lora_tile(1, 1, 1, 1)

                with pe.Fori(0, BLOCKS) as blk:
                    st = STAGES_BLOCK * blk
                    gate_or_up(0, 2 * blk + 1, S_GATE1 + st, 4 * blk + 2, 0)
                    gate_or_up(1, 2 * blk + 1, S_BLOCK + 1 + st, 4 * blk + 3, 1)
                    gate_or_up(0, 2 * blk + 2, S_BLOCK + 2 + st, 4 * blk + 4, 0)
                    stages_ready(S_BLOCK + 3 + st)
                    pe.wait_ge(act_split, 4 * (BLOCKS + 1) * half + 4 * blk + 4)
                    for g in range(1 + KT):
                        p, use = (2, 5 * blk + 1 + g // 2) if g % 2 == 0 else (3, 4 * blk + g // 2)
                        banks_free(p, use)
                        for t in range(2):
                            if g == 0:
                                lora_down(p, t, tail=False)
                            else:
                                down_product(p, g - 1, t, tail=False, stop=(t == 1))
                    gate_or_up(1, 2 * blk + 2, S_BLOCK + 4 + st, 4 * blk + 5, 1)

                stages_ready(S_DOWN_LAST - 1)
                width_product(0, U_TAIL, 1, stop=False)
                lora_tile(0, LB - 2, 0, 0, last=False)
                lora_tile(0, LB - 1, 1, 1)
                b_down_w = wt[0:3 * 2 * RANK, 1, :, :, :].rearrange("p c k m -> p c (k m)")

                def last_first(j):
                    p, use = last_block(j)
                    banks_free(p, use)
                    if j == 0:
                        lora_down(p, 0, tail=False)
                    else:
                        down_product(p, j - 1, 0, tail=False, stop=False)

                def last_second(j):
                    p, _ = last_block(j)
                    if j == 0:
                        lora_down(p, 1, tail=True)
                    else:
                        down_product(p, j - 1, 1, tail=True, stop=False)

                def last_lora(j):
                    p, _ = last_block(j)
                    for chunk in range(CHUNKS):
                        nc.tensor.matmul(pair[p][:, chunk, :], b_down_w[:, chunk, (j - 1) * P:j * P],
                                         ranks[:, chunk, 0, :], start=False, stop=True).then_inc(groups_done, 1)

                stages_ready(S_DOWN_LAST)
                pe.wait_ge(act_split, 4 * (BLOCKS + 1) * half + 4 * BLOCKS + 2)
                for j in range(4):
                    last_first(j)
                stages_ready(S_DOWN_TAIL)
                pe.wait_ge(act_split, 4 * (BLOCKS + 1) * half + 4 * BLOCKS + 4)
                for j in range(4):
                    last_second(j)
                last_first(4)
                last_second(4)
                stages_ready(S_BDOWN + 1)
                pe.wait_ge(lora_split, 4 * half + 4)
                for j in range(1, 5):
                    last_lora(j)
                for j in range(5, KT + 1):
                    last_first(j)
                    last_second(j)
                    last_lora(j)

                pe.wait_ge(route_ready, 1)
                banks_free(3, U_ROUTER)
                for a in (HI, LO):
                    for k in range(KT):
                        if a == HI:
                            pe.wait_ge(x_rounded, 2 * KT * half + KT + k + 1)
                        elif k == 0:
                            pe.wait_ge(x0_split, half + 1)
                        else:
                            pe.wait_ge(x_split, SPLITS_X * half + KT + k)
                        for chunk in range(CHUNKS):
                            last = k == KT - 1 and a == LO
                            mm = nc.tensor.matmul(pair[3][0:2 * EXPERTS, chunk, :],
                                                  route_w[:, k, :, :].rearrange("p a e -> p (a e)"),
                                                  xs[a][:, k, columns(chunk)],
                                                  start=(k == 0 and a == HI), stop=last)
                            if last:
                                mm.then_inc(groups_done, 1)
                stages_ready(S_EXPERTS)

                def before_transposes():
                    pe.wait_ge(pair_free[3], freed(3, half, U_ROUTER))
                    banks_free(0, U_LOGITS_T)

                width_product(1, U_EXPERTS, 0, stop=True, also_wait=before_transposes)
                per_chunk = TT // CHUNKS
                for chunk in range(CHUNKS):
                    for t in range(per_chunk):
                        mm = nc.tensor.transpose(pair[0][:, chunk, t * 2 * EXPERTS:(t + 1) * 2 * EXPERTS],
                                                 tmp_s[0:2 * EXPERTS, chunk, t * P:(t + 1) * P],
                                                 ident[0:2 * EXPERTS, 0:2 * EXPERTS])
                    mm.then_inc(groups_done, 1)

                def out_main(o):
                    p, use = out_tile(o)
                    stages_ready(S_OUT + o)
                    width_product(p, use, (o + 1) % 2, stop=False)

                def out_lora(o):
                    p, use = out_tile(o)
                    if o == 0:
                        pe.wait_ge(hg_split, 2 * half + 2)
                    if o == KT - 1:
                        banks_free(p, use)
                    for w, a in PASSES:
                        for chunk in range(CHUNKS):
                            last = w == LO and o < KT - 1
                            mm = nc.tensor.matmul(pair[p][:, chunk, :], wd[:, 0, w, o * P:(o + 1) * P],
                                                  act[:, 0, a, columns(chunk)],
                                                  start=(o == KT - 1 and (w, a) == (HI, HI)), stop=last)
                            if last:
                                mm.then_inc(groups_done, 1)

                out_main(0)
                pe.wait_ge(route_step, ROUTE_STEPS * half + ROUTE_STEPS)
                banks_free(0, U_GATES_T)
                for chunk in range(CHUNKS):
                    for t in range(per_chunk):
                        mm = nc.tensor.transpose(pair[0][:, chunk, t * P:(t + 1) * P],
                                                 tmp_p[:, chunk, t * P:(t + 1) * P], ident[:, :])
                    mm.then_inc(groups_done, 1)
                out_main(1)
                out_lora(0)
                out_lora(1)
                for o in range(2, KT - 1):
                    out_main(o)
                    out_lora(o)
                out_lora(KT - 1)
                p, _ = out_tile(KT - 1)
                stages_ready(S_OUT + KT - 1)
                order = ([(k, chunk) for k in range(KT // 2) for chunk in range(CHUNKS)]
                         + [(k, chunk) for chunk in range(CHUNKS) for k in range(KT // 2, KT)])
                for k, chunk in order:
                    for w, a in PASSES:
                        mm = nc.tensor.matmul(pair[p][:, chunk, :], wt[:, KT % 2, w, k, :], xs[a][:, k, columns(chunk)],
                                              start=False, stop=(k == KT - 1 and w == LO))
                    if k == KT - 1:
                        mm.then_inc(groups_done, 1)
                    elif chunk == CHUNKS - 1:
                        mm.then_inc(xs_free, 1)

        @block.scalar
        def _(sc):
            def copy(dst, src, **kw):
                return nc.scalar.activation(dst, src, ACT.Copy, **kw)

            sc.sem_inc(pair_free[0], 2)
            sc.dma_start(adapters[:, :], adapter_of).then_inc(adapters_in, 16)
            with sc.Fori(0, HALVES) as half:
                stage0 = STAGES * half

                def arrived(k, base):
                    h, blk = base
                    sc.wait_ge(stage_in[k % RING],
                               LOADED * (STAGES // RING) * h + LOADED * (STAGES_BLOCK // RING) * blk
                               + LOADED * (k // RING + 1))

                def round_wt(k, blk, slot, free_at):
                    sc.wait_ge(groups_done, free_at)
                    arrived(k, (half, blk))
                    copy(wt[:, slot, HI, :, :].rearrange("p k m -> p (k m)"), stage[:, k % RING, :]
                         ).then_inc(rounded, 1)

                def round_lb(slot, e, in_count):
                    sc.wait_ge(lb_in[slot], in_count)
                    copy(lbw[:, slot, :, :], lb_raw[:, slot, :, :]).then_inc(lb_rounded, 1)

                def lb_count(e_half, blk=0):
                    return 48 * (LB // 2) * half + 48 * 2 * blk + 48 * (e_half // 2 + 1)

                def round_wd(k, blk, t, free_at, tile):
                    sc.wait_ge(groups_done, free_at)
                    arrived(k, (half, blk))
                    copy(wd[:, t, HI, :], stage[:, k % RING, :])
                    sc.wait_ge(ad_in, 64 * half + 64)
                    copy(ad[:, t, :].rearrange("p (c a b r) -> p c a b r", c=CHUNKS, a=2, b=2)[:, :, HI, :, :],
                         ad_raw[:, :, bass.ds(tile, 1), :].rearrange("p (c b) o r -> p c b (o r)", c=CHUNKS)
                         ).then_inc(rounded, 1)

                def silu(group, use, s_free):
                    for chunk in range(CHUNKS):
                        sc.wait_ge(groups_done, done(half, group, chunk))
                        sc.wait_ge(pair_free[1], free_for(1, half, s_free, chunk))
                        nc.scalar.activation(tmp_s[:, chunk, :], pair[0][:, chunk, :], ACT.Silu
                                             ).then_inc(pair_free[0], 1)

                def round_act(t, up_use):
                    for chunk in range(CHUNKS):
                        sc.wait_ge(pair_free[1], freed(1, half, up_use, chunk))
                        copy(act[:, t, HI, chunk * CH:(chunk + 1) * CH], tmp_p[:, chunk, :]
                             ).then_inc(act_rounded, 1)

                def round_x(k):
                    if k < KT - 1:
                        sc.wait_ge(xs_free, (KT - 1) * half + k + 1)
                    sc.wait_ge(x_in[k], 16 * half + 16)
                    copy(xs[HI][:, k, :], resid[:, k, :]).then_inc(x_rounded, 1)

                round_wt(S_GATE0, 0, 1, done_last_half(half, G_OUT + KT - 2))
                for k in range(RANKS_AT):
                    round_x(k)
                sc.wait_ge(groups_done, done_last_half(half, G_OUT + KT - 1))
                arrived(S_RANK, (half, 0))
                rank_w = wt[:, 0, :, :, :].rearrange("p c k (a g b r) -> p c k a g b r", a=2, g=2, b=2)
                raw = stage[:, S_RANK, :].rearrange("p (c b k g r) -> p c b k g r", c=CHUNKS, b=2, k=KT, g=2)
                for chunk in range(CHUNKS):
                    for b in range(2):
                        last = copy(rank_w[:, chunk, :, HI, :, b, :], raw[:, chunk, b, :, :, :])
                last.then_inc(rounded, 1)
                for k in range(RANKS_AT, KT):
                    round_x(k)
                round_wt(S_UP0, 0, 0, done(half, G_RANK))
                sc.wait_ge(const_in, 16 * 5)
                for chunk in range(CHUNKS):
                    sc.wait_ge(groups_done, done(half, G_RANK, chunk))
                    for b in range(2):
                        cols = slice(b * SEQ, (b + 1) * SEQ)
                        last = copy(tmp_s[0:64, chunk, cols], pair[2][64:128, chunk, cols],
                                    scale=scale_of[64:128, b:b + 1])
                    last.then_inc(lora_lo, 1)
                for chunk in range(CHUNKS):
                    sc.wait_ge(pair_free[2], freed(2, half, 0, chunk))
                    copy(ranks[0:32, chunk, 0, :], tmp_p[0:32, chunk, :]).then_inc(lora_rounded, 1)
                    copy(ranks[64:96, chunk, 0, :], tmp_p[0:32, chunk, :]).then_inc(lora_rounded, 1)
                round_lb(0, 0, lb_count(0))
                round_lb(1, 1, lb_count(1))
                round_wt(S_GATE1, 0, 1, done(half, G_GATE0))
                silu(G_GATE0, 0, 0)
                round_lb(0, 2, lb_count(2))

                with sc.Fori(0, BLOCKS) as blk:
                    g = PER_BLOCK * blk + G_BLOCK
                    round_wd(S_BLOCK, blk, 0, done(half, g - 1), 2 * blk)
                    round_act(0, 2 * blk)
                    round_wt(S_BLOCK + 1, blk, 0, done(half, g + G_UP_A))
                    round_lb(1, 3, lb_count(3, blk))
                    silu(g + G_GATE_B, 2 * blk + 1, 2 * blk + 1)
                    round_wt(S_BLOCK + 2, blk, 1, done(half, g + G_GATE_B))
                    round_lb(0, 4, lb_count(4, blk))
                    round_wd(S_BLOCK + 3, blk, 1, done(half, g - 1), 2 * blk + 1)
                    round_act(1, 2 * blk + 1)
                    round_wt(S_BLOCK + 4, blk, 0, done(half, g + G_UP_B))
                    round_lb(1, 5, lb_count(5, blk))
                    silu(g + G_GATE_NEXT, 2 * blk + 2, 2 * blk + 2)
                    round_wt(S_BLOCK + 5, blk, 1, done(half, g + G_GATE_NEXT))
                    round_lb(0, 6, lb_count(6, blk))

                round_wd(S_DOWN_LAST, 0, 0, done(half, G_UP_LAST - 1), FULL - 1)
                round_act(0, 2 * BLOCKS)
                sc.wait_ge(groups_done, done(half, G_UP_LAST))
                round_lb(1, LB - 1, lb_count(LB - 1))
                round_wd(S_DOWN_TAIL, 0, 1, done(half, G_UP_LAST - 1), FULL)
                for chunk in range(CHUNKS):
                    sc.wait_ge(groups_done, done(half, G_TAIL, chunk))
                    sc.wait_ge(act_split, 4 * (BLOCKS + 1) * half + 4 * BLOCKS + chunk + 1)
                    nc.scalar.activation(tmp_s[0:TAIL, chunk, :], pair[0][0:TAIL, chunk, :], ACT.Silu)
                    copy(tmp_p[0:TAIL, chunk, :], pair[0][TAIL:2 * TAIL, chunk, :]).then_inc(pair_free[0], 1)
                for chunk in range(CHUNKS):
                    sc.wait_ge(tail_product, 2 * half + chunk + 1)
                    copy(act[0:TAIL, 1, HI, chunk * CH:(chunk + 1) * CH], tmp_p[0:TAIL, chunk, :]
                         ).then_inc(act_rounded, 1)
                b_down_w = wt[0:3 * 2 * RANK, 1, :, :, :].rearrange("p c k m -> p c (k m)")
                sc.wait_ge(groups_done, done(half, G_TAIL))
                for chunk in range(CHUNKS):
                    arrived(S_BDOWN + chunk, (half, 0))
                    copy(b_down_w[:, chunk, :], stage[0:3 * 2 * RANK, (S_BDOWN + chunk) % RING, :]
                         ).then_inc(rounded, 1)
                for chunk in range(CHUNKS):
                    rows, low = slice(64 * chunk, 64 * chunk + 32), slice(64 * chunk + 32, 64 * chunk + 64)
                    sc.wait_ge(pair_free[2], freed(2, half, FIRST4[2], chunk))
                    for b in range(2):
                        cols = slice(b * SEQ, (b + 1) * SEQ)
                        last = copy(tmp_s[rows, chunk, cols], ldown[low, cols], scale=scale_of[low, b:b + 1])
                    last.then_inc(lora_lo, 1)
                for chunk in range(CHUNKS):
                    rows = slice(64 * chunk, 64 * chunk + 32)
                    sc.wait_ge(lora_sum, 2 * half + chunk + 1)
                    copy(ranks[rows, chunk, 0, :], tmp_p[rows, chunk, :]).then_inc(lora_rounded, 1)
                round_wt(S_EXPERTS, 0, 0, done(half, G_UP_LAST))
                for k in range(KT):
                    p, use = last_block(k + 1)
                    sc.wait_ge(pair_free[p], freed(p, half, use))
                    copy(xs[HI][:, k, :], resid[:, k, :]).then_inc(x_rounded, 1)
                sc.wait_ge(groups_done, done(half, G_DOWN_LAST + KT - 1))
                arrived(S_EXPERTS_B, (half, 0))
                copy(wd[:, 0, HI, :], stage[:, S_EXPERTS_B % RING, :]).then_inc(rounded, 1)
                round_wt(S_OUT, 0, 1, done(half, G_DOWN_LAST + KT - 1))
                for chunk in range(CHUNKS):
                    sc.wait_ge(groups_done, done(half, G_ROUTER, chunk))
                    copy(tmp_s[0:2 * EXPERTS, chunk, :], pair[3][0:2 * EXPERTS, chunk, :]).then_inc(pair_free[3], 1)
                round_wt(S_OUT + 1, 0, 0, done(half, G_EXPERTS))
                per_chunk = TT // CHUNKS
                for chunk in range(CHUNKS):
                    sc.wait_ge(groups_done, done(half, G_LOGITS_T, chunk))
                    copy(logits2[:, chunk * per_chunk:(chunk + 1) * per_chunk, :, :].rearrange("p t a e -> p (t a e)"),
                         pair[0][:, chunk, 0:per_chunk * 2 * EXPERTS]).then_inc(pair_free[0], 1)
                sc.wait_ge(route_step, ROUTE_STEPS * half + 4)
                nc.scalar.activation(odds[:, 1, :], odds[:, 0, :], ACT.Exp).then_inc(exp_ready, 1)
                for chunk in range(CHUNKS):
                    sc.wait_ge(groups_done, done(half, G_GATES_T, chunk))
                    copy(tmp_s[:, chunk, :], pair[0][:, chunk, :]).then_inc(pair_free[0], 1)
                round_wt(S_OUT + 2, 0, 1, done(half, G_GATES_T))
                for chunk in range(CHUNKS):
                    sc.wait_ge(pair_free[1], freed(1, half, U_EXPERTS, chunk))
                    copy(act[:, 0, HI, chunk * CH:(chunk + 1) * CH], tmp_p[:, chunk, :]).then_inc(hg_rounded, 1)
                for o in range(3, KT):
                    round_wt(S_OUT + o, 0, (o + 1) % 2, done(half, G_OUT + o - 2))

        @block.vector
        def _(dve):
            def rest(dst, whole, high):
                return nc.vector.tensor_tensor(dst, whole, high.bitcast(F32), ALU.subtract)

            dve.sem_inc(split, RING)
            dve.sem_inc(lb_split, 2)
            for p in range(1, 4):
                dve.sem_inc(pair_free[p], 2)

            with dve.Fori(0, HALVES) as half:
                stage0 = STAGES * half

                def rounded_by(n):
                    return STAGES * half + n + 1

                def rest_wt(k, n, slot):
                    dve.wait_ge(rounded, rounded_by(n))
                    rest(wt[:, slot, LO, :, :].rearrange("p k m -> p (k m)"), stage[:, k % RING, :],
                         wt[:, slot, HI, :, :].rearrange("p k m -> p (k m)")).then_inc(split, 1)

                def rest_lb(slot, e):
                    rows = slice(4 * RANK, 6 * RANK)
                    dve.wait_ge(lb_rounded, LB * half + e + 1)
                    rest(lbw[rows, slot, :, :], lb_raw[rows, slot, :, :], lbw[rows, slot, :, :]
                         ).then_inc(lb_split, 1)

                def rest_wd(k, n, t, tile):
                    dve.wait_ge(rounded, rounded_by(n))
                    rest(wd[:, t, LO, :], stage[:, k % RING, :], wd[:, t, HI, :])
                    by_part = ad[:, t, :].rearrange("p (c a b r) -> p c a b r", c=CHUNKS, a=2, b=2)
                    rest(by_part[:, :, LO, :, :],
                         ad_raw[:, :, bass.ds(tile, 1), :].rearrange("p (c b) o r -> p c b (o r)", c=CHUNKS),
                         by_part[:, :, HI, :, :]).then_inc(split, 1)

                def product(group, gate_use):
                    for chunk in range(CHUNKS):
                        dve.wait_ge(pair_free[0], freed(0, half, gate_use, chunk))
                        dve.wait_ge(groups_done, done(half, group, chunk))
                        nc.vector.tensor_tensor(tmp_p[:, chunk, :], tmp_s[:, chunk, :], pair[1][:, chunk, :],
                                                ALU.mult).then_inc(pair_free[1], 1)

                def rest_act(t, n):
                    for chunk in range(CHUNKS):
                        cols = slice(chunk * CH, (chunk + 1) * CH)
                        dve.wait_ge(act_rounded, 4 * (BLOCKS + 1) * half + 2 * n + chunk + 1)
                        rest(act[:, t, LO, cols], tmp_p[:, chunk, :], act[:, t, HI, cols]).then_inc(act_split, 1)

                def add_down(p, group, h):
                    for chunk in range(CHUNKS):
                        cols = slice(chunk * CH, (chunk + 1) * CH)
                        dve.wait_ge(groups_done, done(half, group, chunk))
                        nc.vector.tensor_tensor(resid[:, h, cols], resid[:, h, cols], pair[p][:, chunk, :],
                                                ALU.add).then_inc(pair_free[p], 1)

                def add_ldown(group):
                    for chunk in range(CHUNKS):
                        rows = slice(64 * chunk, 64 * chunk + 64)
                        dve.wait_ge(groups_done, done(half, group, chunk))
                        nc.vector.tensor_tensor(ldown[rows, :], ldown[rows, :], pair[2][rows, chunk, :],
                                                ALU.add).then_inc(pair_free[2], 1)

                def rest_x(n):
                    k = n % KT
                    dve.wait_ge(x_rounded, 2 * KT * half + n + 1)
                    rest(xs[LO][:, k, :], resid[:, k, :], xs[HI][:, k, :]).then_inc(x_split, 1)

                rest_wt(S_GATE0, S_GATE0, 1)
                for k in range(EARLY):
                    rest_x(k)
                for k in range(EARLY, KT):
                    rest_x(k)
                nc.vector.memset(ldown[:, :], 0.0).then_inc(ldown_cleared, 1)
                dve.wait_ge(split, STAGES * half + S_UP0 + RING)
                rest_wt(S_UP0, S_UP0, 0)
                for chunk in range(CHUNKS):
                    dve.wait_ge(lora_lo, 4 * half + chunk + 1)
                    dve.wait_ge(groups_done, done(half, G_RANK, chunk))
                    for b in range(2):
                        cols = slice(b * SEQ, (b + 1) * SEQ)
                        last = nc.vector.scalar_tensor_tensor(
                            out=tmp_p[0:64, chunk, cols], in0=pair[2][0:64, chunk, cols], scalar=scale_of[0:64, b:b + 1],
                            in1=tmp_s[0:64, chunk, cols], op0=ALU.mult, op1=ALU.add)
                    last.then_inc(pair_free[2], 1)
                for chunk in range(CHUNKS):
                    dve.wait_ge(pair_free[2], freed(2, half, 0, chunk))
                    nc.vector.tensor_copy(ranks[32:64, chunk, 1, :], tmp_p[32:64, chunk, :]).then_inc(lora_up_rounded, 1)
                    nc.vector.tensor_copy(ranks[64:96, chunk, 1, :], tmp_p[32:64, chunk, :])
                    dve.wait_ge(lora_rounded, 6 * half + 2 * chunk + 1)
                    rest(ranks[32:64, chunk, 0, :], tmp_p[0:32, chunk, :], ranks[0:32, chunk, 0, :])
                    dve.wait_ge(lora_rounded, 6 * half + 2 * chunk + 2)
                    dve.wait_ge(lora_up_rounded, 2 * half + chunk + 1)
                    rest(ranks[0:32, chunk, 1, :], tmp_p[32:64, chunk, :], ranks[32:64, chunk, 1, :]
                         ).then_inc(lora_split, 1)
                rest_lb(0, 0)
                rest_lb(1, 1)
                rest_wt(S_GATE1, S_GATE1, 1)
                rest_lb(0, 2)

                with dve.Fori(0, BLOCKS) as blk:
                    st = STAGES_BLOCK * blk
                    g = PER_BLOCK * blk + G_BLOCK
                    rest_wd(S_BLOCK, S_BLOCK + st, 0, 2 * blk)
                    product(g + G_UP_A, 2 * blk)
                    rest_act(0, 2 * blk)
                    rest_wt(S_BLOCK + 1, S_BLOCK + 1 + st, 0)
                    rest_lb(1, 4 * blk + 3)
                    rest_wt(S_BLOCK + 2, S_BLOCK + 2 + st, 1)
                    rest_lb(0, 4 * blk + 4)
                    rest_wd(S_BLOCK + 3, S_BLOCK + 3 + st, 1, 2 * blk + 1)
                    product(g + G_UP_B, 2 * blk + 1)
                    rest_act(1, 2 * blk + 1)
                    rest_wt(S_BLOCK + 4, S_BLOCK + 4 + st, 0)
                    rest_lb(1, 4 * blk + 5)
                    dve.wait_ge(ldown_cleared, half + 1)
                    dve.wait_ge(pair_free[2], free_for(2, half, 5 * blk + 1))
                    dve.wait_ge(pair_free[3], free_for(3, half, 4 * blk))
                    add_ldown(g + G_LDOWN)
                    for h in range(KT):
                        add_down(3 - h % 2, g + G_DOWN + h, h)
                        if h == 1:
                            rest_wt(S_BLOCK + 5, S_BLOCK + 5 + st, 1)
                            rest_lb(0, 4 * blk + 6)

                rest_wd(S_DOWN_LAST, S_DOWN_LAST, 0, FULL - 1)
                product(G_UP_LAST, 2 * BLOCKS)
                rest_act(0, 2 * BLOCKS)
                rest_lb(1, LB - 1)
                rest_wd(S_DOWN_TAIL, S_DOWN_TAIL, 1, FULL)
                for chunk in range(CHUNKS):
                    dve.wait_ge(pair_free[0], freed(0, half, U_TAIL, chunk))
                    nc.vector.tensor_tensor(tmp_p[0:TAIL, chunk, :], tmp_s[0:TAIL, chunk, :],
                                            tmp_p[0:TAIL, chunk, :], ALU.mult).then_inc(tail_product, 1)
                for chunk in range(CHUNKS):
                    cols = slice(chunk * CH, (chunk + 1) * CH)
                    dve.wait_ge(act_rounded, 4 * (BLOCKS + 1) * half + 4 * BLOCKS + 2 + chunk + 1)
                    rest(act[TAIL:2 * TAIL, 1, HI, cols], tmp_p[0:TAIL, chunk, :], act[0:TAIL, 1, HI, cols]
                         ).then_inc(act_split, 1)
                dve.wait_ge(pair_free[2], free_for(2, half, FIRST4[2]))
                dve.wait_ge(pair_free[3], free_for(3, half, FIRST4[3]))
                add_ldown(G_LDOWN_LAST)
                for chunk in range(CHUNKS):
                    rows = slice(64 * chunk, 64 * chunk + 32)
                    dve.wait_ge(lora_lo, 4 * half + 2 + chunk + 1)
                    for b in range(2):
                        cols = slice(b * SEQ, (b + 1) * SEQ)
                        last = nc.vector.scalar_tensor_tensor(
                            out=tmp_p[rows, chunk, cols], in0=ldown[rows, cols], scalar=scale_of[rows, b:b + 1],
                            in1=tmp_s[rows, chunk, cols], op0=ALU.mult, op1=ALU.add)
                    last.then_inc(lora_sum, 1)
                for chunk in range(CHUNKS):
                    rows = slice(64 * chunk, 64 * chunk + 32)
                    other = slice(64 * (1 - chunk), 64 * (1 - chunk) + 32)
                    dve.wait_ge(lora_sum, 2 * half + chunk + 1)
                    nc.vector.tensor_copy(ranks[other, chunk, 0, :], tmp_p[rows, chunk, :])
                    dve.wait_ge(lora_rounded, 6 * half + 4 + chunk + 1)
                    rest(ranks[32:64, chunk, 0, :], tmp_p[rows, chunk, :], ranks[rows, chunk, 0, :]
                         ).then_inc(lora_split, 1)
                for h in range(KT):
                    add_down(last_block(h + 1)[0], G_DOWN_LAST + h, h)
                    if h > 3:
                        rest_x(KT + h - 3)
                for h in range(KT - 3, KT):
                    rest_x(KT + h)
                dve.wait_ge(split, STAGES * half + S_EXPERTS_B + RING)
                dve.wait_ge(rounded, rounded_by(S_EXPERTS_B))
                rest(wd[:, 0, LO, :], stage[:, S_EXPERTS_B % RING, :], wd[:, 0, HI, :]).then_inc(split, 1)
                rest_wt(S_OUT, S_OUT, 1)
                rest_wt(S_OUT + 1, S_OUT + 1, 0)

                def link(instruction, step):
                    instruction.then_inc(route_step, 1)
                    if step < ROUTE_STEPS:
                        dve.wait_ge(route_step, ROUTE_STEPS * half + step)

                def over(ap, n):
                    return ap.unsqueeze(ap.ndim).to_broadcast(list(ap.shape) + [n])

                dve.wait_ge(bias_ready, 1)
                dve.wait_ge(pair_free[0], freed(0, half, U_LOGITS_T))
                link(nc.vector.tensor_tensor(logits[:, :, :], logits2[:, :, HI, :], logits2[:, :, LO, :], ALU.add), 1)
                for t in range(TT // SEQ_HALF):
                    by_seq = logits[:, :, :].rearrange("p (s t) e -> p s t e", t=TT // SEQ_HALF)[:, :, t, :]
                    last = nc.vector.tensor_tensor(by_seq, by_seq, lang_bias[:, bass.ds(SEQ_HALF * half, SEQ_HALF), :],
                                                   ALU.add)
                link(last, 2)
                nc.vector.tensor_reduce(highest[:, :], logits[:, :, :], mybir.AxisListType.X, ALU.max)
                for t in range(TT):
                    last = nc.vector.max(best[:, t, :], logits[:, t, :])
                link(last, 3)
                nc.vector.tensor_tensor(odds[:, 0, :], best[:, :, 1], highest[:, :], ALU.subtract
                                        ).then_inc(route_step, 1)
                for t in range(TT):
                    last = nc.vector.max_index(best_at[:, t, :], best[:, t, :], logits[:, t, :])
                link(last, 5)
                nc.vector.tensor_copy(best_no[:, :, :], best_at[:, :, 0:2])
                dve.wait_ge(exp_ready, half + 1)
                link(nc.vector.tensor_scalar(weight[:, 0, :], odds[:, 1, :], 1.0, None, ALU.add), 6)
                link(nc.vector.reciprocal(weight[:, 1, :], weight[:, 0, :]), 7)
                link(nc.vector.tensor_scalar(weight[:, 2, :], weight[:, 1, :], SCALING, None, ALU.mult), 8)
                nc.vector.tensor_tensor(weight[:, 3, :], weight[:, 2, :], odds[:, 1, :], ALU.mult)
                numbers = expert[:, :].unsqueeze(1).to_broadcast([P, TT, EXPERTS])
                for i in range(2):
                    last = nc.vector.tensor_tensor(picked[:, i, :, :], numbers, over(best_no[:, :, i], EXPERTS),
                                                   ALU.is_equal)
                link(last, 9)
                for i in range(2):
                    last = nc.vector.tensor_tensor(picked[:, i, :, :], picked[:, i, :, :],
                                                   over(weight[:, 2 + i, :], EXPERTS), ALU.mult)
                link(last, 10)
                by_token = picked[:, :, :, :].rearrange("p i t e -> p i (t e)")
                link(nc.vector.tensor_tensor(
                    tmp_p[:, :, :].rearrange("p c n -> p (c n)").rearrange("p (n r) -> p n r", r=RANK),
                    over(by_token[:, 0, :], RANK), over(by_token[:, 1, :], RANK), ALU.add), 11)

                for chunk in range(CHUNKS):
                    dve.wait_ge(pair_free[0], freed(0, half, U_GATES_T, chunk))
                    nc.vector.tensor_tensor(tmp_p[:, chunk, :], tmp_s[:, chunk, :], pair[1][:, chunk, :],
                                            ALU.mult).then_inc(pair_free[1], 1)
                for chunk in range(CHUNKS):
                    cols = slice(chunk * CH, (chunk + 1) * CH)
                    dve.wait_ge(hg_rounded, 2 * half + chunk + 1)
                    rest(act[:, 0, LO, cols], tmp_p[:, chunk, :], act[:, 0, HI, cols]).then_inc(hg_split, 1)
                rest_wt(S_OUT + 2, S_OUT + 2, 1)
                for o in range(KT):
                    if o + 3 < KT:
                        rest_wt(S_OUT + o + 3, S_OUT + o + 3, o % 2)
                    add_down(RING3[o % 3], G_OUT + o, o)


_OUT = (HALVES, KT, P, NT)


def kernel(**inputs):
    import numpy as np
    import concourse.bacc as bacc
    from concourse.bass_utils import run_bass_kernel_spmd

    v = {name: np.asarray(a) for name, a in inputs.items()}

    def width_tiles(w):
        return np.ascontiguousarray(w.reshape(-1, P, KT, P).transpose(0, 3, 2, 1)).reshape(-1, P, D)

    gate, up = v["L0_cond_W_gate"], v["L0_cond_W_up"]
    full = FULL * P
    pairs = np.stack([gate[:full].reshape(FULL, P, D), up[:full].reshape(FULL, P, D)], 1).reshape(-1, D)
    w_gu = width_tiles(np.concatenate([pairs, gate[full:], up[full:]]))
    down_t = v["L0_cond_W_down"].T
    w_down = np.concatenate([down_t, down_t[full:]]).reshape(FT, P, D)
    a_g, a_u = v["L0_cond_A_gate"][0], v["L0_cond_A_up"][0]
    a_gu = np.stack([a_g, a_u], 1).reshape(ADAPTERS, 2, RANK, KT, P).transpose(0, 4, 3, 1, 2).reshape(ADAPTERS, P, -1)
    b_g, b_u = (v[n][0].transpose(0, 2, 1) for n in ("L0_cond_B_gate", "L0_cond_B_up"))
    b_gu = np.zeros((ADAPTERS, RANK, LB, P), b_g.dtype)
    b_gu[:, :, 0:2 * FULL:2] = b_g[:, :, :full].reshape(ADAPTERS, RANK, FULL, P)
    b_gu[:, :, 1:2 * FULL:2] = b_u[:, :, :full].reshape(ADAPTERS, RANK, FULL, P)
    b_gu[:, :, LB - 2, :TAIL] = b_g[:, :, full:]
    b_gu[:, :, LB - 1, TAIL:] = b_u[:, :, full:]
    a_d = v["L0_cond_A_down"][0]
    a_down = np.concatenate([a_d, a_d[:, :, full:]], 2).reshape(ADAPTERS, RANK, FT, P)
    a_down = a_down.transpose(0, 3, 2, 1).reshape(ADAPTERS, P, FT * RANK)
    tokens = v["x"].reshape(HALVES, NT, KT, P)
    rows = np.arange(P)
    arrays = {
        "x_t": tokens.transpose(0, 2, 3, 1),
        "w_gu": w_gu,
        "w_down": w_down,
        "a_gu": a_gu,
        "b_gu": b_gu,
        "a_down": a_down,
        "b_down": v["L0_cond_B_down"][0].transpose(0, 2, 1),
        "w_out": width_tiles(v["L1_cond_W"]),
        "a_exp": width_tiles(v["L1_cond_A"].reshape(EXPERTS * RANK, D))[0],
        "b_exp": v["L1_cond_B"].transpose(0, 2, 1).reshape(EXPERTS * RANK, D),
        "w_route": v["L1_cond_Wr"].reshape(EXPERTS, KT, P).transpose(2, 1, 0),
        "adapter_of": v["itok_B_2_6"].reshape(1, NSEQ),
        "language_of": v["itok_B_0_7"].reshape(1, NSEQ),
        "identity": np.eye(P, dtype=np.float32),
        "seq_scale": np.stack([np.where(rows // RANK % 2 == b, LORA_SCALE, 0.0) for b in range(2)], 1).astype(np.float32),
        "expert_no": np.tile(np.arange(EXPERTS, dtype=np.float32), (P, 1)),
    }
    arrays = {name: np.ascontiguousarray(a) for name, a in arrays.items()}
    nc = bacc.Bacc("TRN2", target_bir_lowering=False, num_devices=1)
    args = [nc.dram_tensor(n, a.shape, mybir.dt.from_np(a.dtype), kind="ExternalInput").ap() for n, a in arrays.items()]
    args.append(nc.dram_tensor("out", _OUT, F32, kind="ExternalOutput").ap())
    cond_resid_kernel(nc, *args)
    got = run_bass_kernel_spmd(nc, [arrays], core_ids=[0]).results[0]["out"]
    return np.ascontiguousarray(got.transpose(0, 3, 1, 2)).reshape(NSEQ, SEQ, D)
```
